# Optimizing a Trainium2 kernel written in Bass

```python
import numpy as np
import jax
import jax.numpy as jnp

def _softmax(x, axis=-1):
    return jax.nn.softmax(x, axis=axis)

def _gelu(x):
    return jax.nn.gelu(x, approximate=True)

def _silu(x):
    return jax.nn.silu(x)

def _sigmoid(x):
    return jax.nn.sigmoid(x)

def _layernorm(x, axis=-1, eps=1e-05):
    m = jnp.mean(x, axis=axis, keepdims=True)
    v = jnp.var(x, axis=axis, keepdims=True)
    return (x - m) / jnp.sqrt(v + eps)

def _scatter_add(tgt, idx, src, axis=0):
    return tgt.at[idx].add(src)

def _segment_sum(src, seg, n):
    return jax.ops.segment_sum(src, seg, n)
kernel_name = 'mk_cond_resid_d4_seqx_r8_ca354c'

def setup_inputs(seed: int=0):
    np.random.seed(seed)
    _w = jnp.asarray

    def _rec_inputs():
        import jax
        import jax.numpy as jnp
        _rk = jax.random.key(seed)
        x = -0.0002071 + 1 * jax.random.normal(jax.random.fold_in(_rk, 1), (2, 512, 128), jnp.float32)
        _lenS = 512 - jax.random.randint(jax.random.fold_in(_rk, 7), (2,), 0, max(1, 512 // 4) + 1, jnp.int32)
        _lenS2 = 512 - jax.random.randint(jax.random.fold_in(_rk, 8), (2,), 0, max(1, 512 // 4) + 1, jnp.int32)
        cond_8 = jax.random.uniform(jax.random.fold_in(_rk, 11), (2, 8), jnp.float32, 0.0, 0.983423)
        return (x, cond_8)
    x, cond_8 = _rec_inputs()

    def _L0_cond_setup():
        import jax, jax.numpy as jnp
        import numpy as np
        R = 16
        ALPHA = 32.0
        SCALING = ALPHA / R
        key = jax.random.key(seed)
        ks = jax.random.split(key, 6)
        B, T, C, O, E = (16, 1500, 128, 128, 8)
        x = jax.random.normal(ks[0], (B, T, C), dtype=jnp.float32)
        w = jax.random.uniform(ks[1], (B, E), dtype=jnp.float32)
        W_base = jax.random.normal(ks[2], (O, C), dtype=jnp.float32) * 0.02
        b_base = jax.random.normal(ks[3], (O,), dtype=jnp.float32) * 0.02
        As = jax.random.normal(ks[4], (E, R, C), dtype=jnp.float32) * 0.02
        Bs = jax.random.normal(ks[5], (E, O, R), dtype=jnp.float32) * 0.02
        return {'x': x, 'w': w, 'W_base': W_base, 'b_base': b_base, 'As': As, 'Bs': Bs}
    _L0_cond_all = _L0_cond_setup()
    _L0_cond_in = {k: v for k, v in _L0_cond_all.items() if k in ('W_base', 'b_base', 'As', 'Bs')}
    del _L0_cond_all

    def _L1_cond_setup():
        import jax, jax.numpy as jnp
        import numpy as np
        TOP_K = 2
        NUM_MOE_LAYERS = 12

        def _gemma_mlp(x, gate_w, up_w, down_w):
            g = jnp.einsum('bsh,hi->bsi', x, gate_w)
            u = jnp.einsum('bsh,hi->bsi', x, up_w)
            return jnp.einsum('bsi,ih->bsh', jax.nn.gelu(g, approximate=True) * u, down_w)
        key = jax.random.key(seed)
        ks = jax.random.split(key, 8)
        B, S, H, I, E = (32, 32, 128, 512, 8)
        std = 0.02
        return {'x': jax.random.normal(ks[0], (B, S, H), jnp.float32), 'router_logits': jax.random.normal(ks[1], (B, E), jnp.float32), 'skill_gate': jax.random.normal(ks[2], (E, H, I), jnp.float32) * std, 'skill_up': jax.random.normal(ks[3], (E, H, I), jnp.float32) * std, 'skill_down': jax.random.normal(ks[4], (E, I, H), jnp.float32) * std, 'shared_gate': jax.random.normal(ks[5], (H, I), jnp.float32) * std, 'shared_up': jax.random.normal(ks[6], (H, I), jnp.float32) * std, 'shared_down': jax.random.normal(ks[7], (I, H), jnp.float32) * std}
    _L1_cond_all = _L1_cond_setup()
    _L1_cond_in = {k: v for k, v in _L1_cond_all.items() if k in ('skill_gate', 'skill_up', 'skill_down', 'shared_gate', 'shared_up', 'shared_down')}
    del _L1_cond_all

    def _L2_cond_setup():
        import jax, jax.numpy as jnp
        import numpy as np
        B, S, D = (16, 256, 128)
        E, H = (8, 256)
        key = jax.random.key(seed)
        ks = jax.random.split(key, 8)
        scale = 0.02
        x = jax.random.normal(ks[0], (B, S, D), dtype=jnp.float32)
        opcode_onehot = jax.random.uniform(ks[1], (B, E), dtype=jnp.float32)
        W_up = jax.random.normal(ks[2], (E, H, D), dtype=jnp.float32) * scale
        b_up = jnp.zeros((E, H), dtype=jnp.float32)
        W_gate = jax.random.normal(ks[3], (E, H, D), dtype=jnp.float32) * scale
        b_gate = jnp.zeros((E, H), dtype=jnp.float32)
        W_down = jax.random.normal(ks[4], (E, D, H), dtype=jnp.float32) * scale
        b_down = jnp.zeros((E, D), dtype=jnp.float32)
        return {'x': x, 'opcode_onehot': opcode_onehot, 'W_up': W_up, 'b_up': b_up, 'W_gate': W_gate, 'b_gate': b_gate, 'W_down': W_down, 'b_down': b_down}
    _L2_cond_all = _L2_cond_setup()
    _L2_cond_in = {k: v for k, v in _L2_cond_all.items() if k in ('W_up', 'b_up', 'W_gate', 'b_gate', 'W_down', 'b_down')}
    del _L2_cond_all

    def _L3_cond_setup():
        import jax, jax.numpy as jnp
        import numpy as np
        key = jax.random.key(seed)
        k1, k2, k3, k4, k5 = jax.random.split(key, 5)
        B, N, T, O, G = (32, 32, 128, 128, 8)
        x = jax.random.normal(k1, (B, N, T), dtype=jnp.float32)
        y = jax.random.uniform(k2, (B, G), dtype=jnp.float32)
        weight = jax.random.normal(k3, (G, O, T), dtype=jnp.float32) * (1.0 / np.sqrt(T))
        mask = jax.random.uniform(k4, (O, T), dtype=jnp.float32)
        bias = jax.random.normal(k5, (O,), dtype=jnp.float32)
        return {'x': x, 'y': y, 'weight': weight, 'mask': mask, 'bias': bias}
    _L3_cond_all = _L3_cond_setup()
    _L3_cond_in = {k: v for k, v in _L3_cond_all.items() if k in ('weight', 'mask', 'bias')}
    del _L3_cond_all
    return {'x': x, 'cond_8': cond_8, 'L0_cond_W_base': _L0_cond_in['W_base'], 'L0_cond_b_base': _L0_cond_in['b_base'], 'L0_cond_As': _L0_cond_in['As'], 'L0_cond_Bs': _L0_cond_in['Bs'], 'L1_cond_skill_gate': _L1_cond_in['skill_gate'], 'L1_cond_skill_up': _L1_cond_in['skill_up'], 'L1_cond_skill_down': _L1_cond_in['skill_down'], 'L1_cond_shared_gate': _L1_cond_in['shared_gate'], 'L1_cond_shared_up': _L1_cond_in['shared_up'], 'L1_cond_shared_down': _L1_cond_in['shared_down'], 'L2_cond_W_up': _L2_cond_in['W_up'], 'L2_cond_b_up': _L2_cond_in['b_up'], 'L2_cond_W_gate': _L2_cond_in['W_gate'], 'L2_cond_b_gate': _L2_cond_in['b_gate'], 'L2_cond_W_down': _L2_cond_in['W_down'], 'L2_cond_b_down': _L2_cond_in['b_down'], 'L3_cond_weight': _L3_cond_in['weight'], 'L3_cond_mask': _L3_cond_in['mask'], 'L3_cond_bias': _L3_cond_in['bias']}

def reference(x, cond_8, L0_cond_W_base, L0_cond_b_base, L0_cond_As, L0_cond_Bs, L1_cond_skill_gate, L1_cond_skill_up, L1_cond_skill_down, L1_cond_shared_gate, L1_cond_shared_up, L1_cond_shared_down, L2_cond_W_up, L2_cond_b_up, L2_cond_W_gate, L2_cond_b_gate, L2_cond_W_down, L2_cond_b_down, L3_cond_weight, L3_cond_mask, L3_cond_bias):
    import jax
    import jax.numpy as jnp

    def _L0_cond_ref(x, w, W_base, b_base, As, Bs):
        import jax, jax.numpy as jnp
        import numpy as np
        R = 16
        ALPHA = 32.0
        SCALING = ALPHA / R
        out = jnp.einsum('btc,oc->bto', x, W_base) + b_base
        h = jnp.einsum('btc,erc->bter', x, As)
        lora = jnp.einsum('bter,eor,be->bto', h, Bs, w)
        return out + lora * SCALING

    def _L1_cond_ref(x, router_logits, skill_gate, skill_up, skill_down, shared_gate, shared_up, shared_down):
        import jax, jax.numpy as jnp
        import numpy as np
        TOP_K = 2
        NUM_MOE_LAYERS = 12

        def _gemma_mlp(x, gate_w, up_w, down_w):
            g = jnp.einsum('bsh,hi->bsi', x, gate_w)
            u = jnp.einsum('bsh,hi->bsi', x, up_w)
            return jnp.einsum('bsi,ih->bsh', jax.nn.gelu(g, approximate=True) * u, down_w)
        B = x.shape[0]
        E = skill_gate.shape[0]
        rw = jax.nn.softmax(router_logits.astype(jnp.float32), axis=-1)
        w, sel = jax.lax.top_k(rw, TOP_K)
        w = w / w.sum(axis=-1, keepdims=True)
        w = w.astype(x.dtype)
        scale = 1.0 / NUM_MOE_LAYERS
        w = scale * w + (1.0 - scale) * jax.lax.stop_gradient(w)
        dense_w = jnp.zeros((B, E), x.dtype).at[jnp.arange(B)[:, None], sel].add(w)

        def step(acc, params):
            g, u, d, we = params
            return (acc + we[:, None, None] * _gemma_mlp(x, g, u, d), None)
        out, _ = jax.lax.scan(step, jnp.zeros_like(x), (skill_gate, skill_up, skill_down, dense_w.T))
        out = out + _gemma_mlp(x, shared_gate, shared_up, shared_down)
        return out

    def _L2_cond_ref(x, opcode_onehot, W_up, b_up, W_gate, b_gate, W_down, b_down):
        import jax, jax.numpy as jnp
        import numpy as np
        B, S, D = (16, 256, 128)
        E, H = (8, 256)
        expert = jnp.argmax(opcode_onehot, axis=-1)
        wu, bu = (W_up[expert], b_up[expert])
        wg, bg = (W_gate[expert], b_gate[expert])
        wd, bd = (W_down[expert], b_down[expert])
        up = jnp.einsum('bsd,bhd->bsh', x, wu) + bu[:, None, :]
        gate = jnp.einsum('bsd,bhd->bsh', x, wg) + bg[:, None, :]
        hidden = jax.nn.silu(up) * gate
        out = jnp.einsum('bsh,bdh->bsd', hidden, wd) + bd[:, None, :]
        return out

    def _L3_cond_ref(x, y, weight, mask, bias):
        import jax, jax.numpy as jnp
        import numpy as np
        masked_w = weight * mask[None, :, :]
        w_bot = jnp.einsum('bg,got->bot', y, masked_w)
        return jnp.einsum('bnt,bot->bno', x, w_bot) + bias
    x = x + _L0_cond_ref(x, cond_8, L0_cond_W_base, L0_cond_b_base, L0_cond_As, L0_cond_Bs)
    x = x + _L1_cond_ref(x, cond_8, L1_cond_skill_gate, L1_cond_skill_up, L1_cond_skill_down, L1_cond_shared_gate, L1_cond_shared_up, L1_cond_shared_down)
    x = x + _L2_cond_ref(x, cond_8, L2_cond_W_up, L2_cond_b_up, L2_cond_W_gate, L2_cond_b_gate, L2_cond_W_down, L2_cond_b_down)
    x = x + _L3_cond_ref(x, cond_8, L3_cond_weight, L3_cond_mask, L3_cond_bias)
    return x

_drawn_inputs = setup_inputs


def setup_inputs(seed=0):
    import zlib

    import numpy as np

    out = dict(_drawn_inputs(seed))
    spreads = {'L2_cond_b_up': (0.0, 0.8), 'L2_cond_b_gate': (0.0, 0.8), 'L2_cond_b_down': (0.0, 0.8)}
    factors = {'L0_cond_b_base': 3.481,
     'L1_cond_skill_gate': 8.0,
     'L1_cond_skill_up': 7.975,
     'L1_cond_skill_down': 7.948,
     'L1_cond_shared_gate': 5.737,
     'L1_cond_shared_up': 5.621,
     'L1_cond_shared_down': 5.619,
     'L2_cond_W_up': 7.593,
     'L2_cond_W_gate': 7.535,
     'L2_cond_W_down': 6.904,
     'L3_cond_bias': 8.0}
    for name, (base, spread) in spreads.items():
        noise = np.random.default_rng([zlib.crc32(name.encode()), seed]).standard_normal(out[name].shape)
        drawn = base * np.exp(spread * noise) if base else spread * noise
        out[name] = jnp.asarray(drawn.astype(out[name].dtype))
    for name, factor in factors.items():
        out[name] = (out[name] * factor).astype(out[name].dtype)
    return out
```

```python
from contextlib import ExitStack

import concourse.bass as bass
from concourse import mybir

ALU = mybir.AluOpType
ACT = mybir.ActivationFunctionType
AX = mybir.AxisListType
F32 = mybir.dt.float32
F32R = mybir.dt.float32r
U32 = mybir.dt.uint32

P = 128
B = 2
T = 512
HALF = T // 2
E = 8
TOP = 2
LORA_SCALE = 2.0
W_SCALE = 1.0 / 12

L1_BLOCKS = 4
L2_BLOCKS = 2
PIECE = 3 * P
L2_BIAS = 2 * L2_BLOCKS + 1

BLOCK_BATCH = [0] * L1_BLOCKS + [1] * L1_BLOCKS + [0] * (TOP * L1_BLOCKS) + [1] * (TOP * L1_BLOCKS)
N1 = len(BLOCK_BATCH)
BLOCK_BATCH += [0] * L2_BLOCKS + [1] * L2_BLOCKS
N = len(BLOCK_BATCH)
NPIECES = N - L1_BLOCKS
PAIRS = 3
HBUFS = 3
LAG = 2
HI_AHEAD = 4


def piece_of(k):
    return k if k < L1_BLOCKS else k - L1_BLOCKS


def is_first(k):
    return k in (0, L1_BLOCKS) or (k >= N1 and (k - N1) % L2_BLOCKS == 0)


def is_last(k):
    return k in (N1 - TOP * L1_BLOCKS - 1, N1 - 1) or (k >= N1 and (k - N1) % L2_BLOCKS == L2_BLOCKS - 1)


def expert_of(k):
    if 2 * L1_BLOCKS <= k < N1:
        n = (k - 2 * L1_BLOCKS) // L1_BLOCKS
        return n // TOP, n % TOP
    return None


def build(nc, x_t, cond, l0, shared, skill, l2, l3, out_t):
    ctx = ExitStack()
    with ctx:
        def sb(name, shape, dt=F32):
            return ctx.enter_context(nc.sbuf_tensor(name, shape, dt))

        def sem(name):
            return ctx.enter_context(nc.semaphore(name))

        x0 = sb("x0", [P, B, T])
        condb = sb("condb", [P, B, E])
        own = sb("own", [P, E])
        picked = sb("picked", [P, B, E])
        wcol = sb("wcol", [P, B])
        params = sb("params", [P, 3 * P + 2])
        a_er, b_er, w_base = params[:, 0:P], params[:, P:2 * P], params[:, 2 * P:3 * P]
        bias0, bias3 = params[:, 3 * P:3 * P + 1], params[:, 3 * P + 1:3 * P + 2]
        bsw = sb("bsw", [P, B, P])
        w_base_i = sb("w_base_i", [P, P])
        w0 = sb("w0", [P, B, P])
        ident = sb("ident", [P, P])
        x1 = sb("x1", [P, B, T])
        x2 = sb("x2", [P, B, T])
        x3 = sb("x3", [P, B, T])
        xhi = sb("xhi", [P, 2, B, T], F32R)
        xlo = sb("xlo", [P, 2, B, T], F32R)
        act = sb("act", [P, 2, T])
        h = sb("h", [P, HBUFS, T])
        hhi = sb("hhi", [P, HBUFS, T], F32R)
        hlo = sb("hlo", [P, HBUFS, T], F32R)
        raw_shared = sb("raw_shared", [P, L1_BLOCKS, PIECE])
        raw_skill = sb("raw_skill", [P, B * TOP, L1_BLOCKS * PIECE])
        raw_l2 = sb("raw_l2", [P, B, L2_BLOCKS * PIECE + L2_BIAS])
        whi = sb("whi", [P, NPIECES, PIECE], F32R)
        wlo = sb("wlo", [P, NPIECES, PIECE], F32R)
        w3in = sb("w3in", [P, E + 1, P])
        w3sum = sb("w3sum", [P, E, P])
        w3 = sb("w3", [P, B, P])
        res = sb("res", [P, B, T])
        warm = sb("warm", [P, T])
        tiny = sb("tiny", [P, 2])
        top = sb("top", [P, B, 8])
        idx = sb("idx", [P, B, 8], U32)
        dif = sb("dif", [P, B, 8])
        ex = sb("ex", [P, B, 8])
        ssum = sb("ssum", [P, B])
        rsum = sb("rsum", [P, B])
        rw = sb("rw", [P, B, TOP])
        pair = sb("pair", [P, B])
        rpair = sb("rpair", [P, B])
        wn = sb("wn", [P, B, TOP])
        wa = sb("wa", [P, B, TOP])
        gate_w = sb("gate_w", [P, B, TOP])

        gp = [ctx.enter_context(nc.psum_tensor(f"gp{i}", [P, T], F32)) for i in range(PAIRS)]
        up = [ctx.enter_context(nc.psum_tensor(f"up{i}", [P, T], F32)) for i in range(PAIRS)]
        acc = [ctx.enter_context(nc.psum_tensor(f"acc{i}", [P, T], F32)) for i in range(B)]
        fold = gp[2][:, 0:B * P].rearrange("p (b c) -> p b c", b=B)
        l3out = [[gp[1][:, :HALF], up[1][:, :HALF]], [gp[2][:, :HALF], up[2][:, :HALF]]]

        ld_cond, ld_par, ld_w3 = sem("ld_cond"), sem("ld_par"), sem("ld_w3")
        ld_x = [sem(f"ld_x{b}") for b in range(B)]
        ld_sh = [sem(f"ld_sh{i}") for i in range(L1_BLOCKS)]
        ld_sk = [sem(f"ld_sk{i}") for i in range(B * TOP)]
        ld_l2 = [sem(f"ld_l2{b}") for b in range(B)]
        s_out = sem("s_out")
        s_warm = sem("s_warm")
        s_ident = sem("s_ident")
        s_own = sem("s_own")
        s_wcol = sem("s_wcol")
        s_wbi = sem("s_wbi")
        s_top = sem("s_top")
        s_idx = sem("s_idx")
        s_dif = sem("s_dif")
        s_exp = sem("s_exp")
        s_rt = sem("s_rt")
        s_bsw = sem("s_bsw")
        s_fold = sem("s_fold")
        s_w0 = sem("s_w0")
        s_l0 = sem("s_l0")
        s_xhi = sem("s_xhi")
        s_xlo = sem("s_xlo")
        s_x1 = sem("s_x1")
        s_x2 = sem("s_x2")
        s_x3 = sem("s_x3")
        s_whi = sem("s_whi")
        s_wlo_sh = sem("s_wlo_sh")
        s_wlo = sem("s_wlo")
        s_g = sem("s_g")
        s_u = sem("s_u")
        s_d = sem("s_d")
        s_act = sem("s_act")
        s_h = sem("s_h")
        s_hhi = sem("s_hhi")
        s_hlo = sem("s_hlo")
        s_f3 = sem("s_f3")
        s_l3o = sem("s_l3o")
        s_resa = sem("s_resa")
        s_resv = sem("s_resv")

        def raw_piece(p):
            if p < L1_BLOCKS:
                return raw_shared[:, p, :]
            q = p - L1_BLOCKS
            if q < B * TOP * L1_BLOCKS:
                i = q % L1_BLOCKS
                return raw_skill[:, q // L1_BLOCKS, i * PIECE:(i + 1) * PIECE]
            q -= B * TOP * L1_BLOCKS
            i = q % L2_BLOCKS
            return raw_l2[:, q // L2_BLOCKS, i * PIECE:(i + 1) * PIECE]

        def wait_piece_loaded(eng, p):
            if p < L1_BLOCKS:
                eng.wait_ge(ld_sh[p], 16)
            elif p < L1_BLOCKS * (1 + B * TOP):
                eng.wait_ge(ld_sk[p // L1_BLOCKS - 1], 16)
            else:
                eng.wait_ge(ld_l2[(p - L1_BLOCKS * (1 + B * TOP)) // L2_BLOCKS], 16)

        block = ctx.enter_context(nc.Block())

        @block.sync
        def _(sp):
            sp.dma_start(params[:, :], l0[:, :]).then_inc(ld_par, 16)
            sp.dma_start(x0[:, 0, :], x_t[:, 0:T]).then_inc(ld_x[0], 16)
            sp.dma_start(raw_shared[:, 0, :], shared[0]).then_inc(ld_sh[0], 16)
            sp.dma_start(x0[:, 1, :], x_t[:, T:2 * T]).then_inc(ld_x[1], 16)
            for i in range(1, L1_BLOCKS):
                sp.dma_start(raw_shared[:, i, :], shared[i]).then_inc(ld_sh[i], 16)
            sp.wait_ge(s_idx, B)
            for b in range(B):
                for r in range(TOP):
                    e = sp.value_load(idx[0:1, b, r:r + 1], min_val=0, max_val=E - 1)
                    n = b * TOP + r
                    sp.dma_start(raw_skill[:, n, :], skill[bass.ds(e, 1), :, :]).then_inc(ld_sk[n], 16)
                    if n == 0:
                        sp.dma_start(w3in[:, :, :], l3.rearrange("p (g o) -> p g o", o=P)).then_inc(ld_w3, 16)
            for b in range(B):
                e = sp.value_load(idx[0:1, b, 0:1], min_val=0, max_val=E - 1)
                sp.dma_start(raw_l2[:, b, :], l2[bass.ds(e, 1), :, :]).then_inc(ld_l2[b], 16)
            for b in range(B):
                sp.wait_ge(s_resv, b + 1)
                sp.dma_start(out_t[:, b * T + HALF:(b + 1) * T], res[:, b, HALF:]).then_inc(s_out, 16)
            sp.wait_ge(s_out, 16 * 2 * B)

        @block.gpsimd
        def _(pool):
            R = P // E
            pool.memset(own[:, :], 1.0).then_inc(s_own, 1)
            pool.wait_ge(s_own, 1)
            pool.affine_select(out=own[:, :], in_=own[:, :], compare_op=ALU.is_ge, fill=0.0,
                               base=0, pattern=[[-R, E]], channel_multiplier=1).then_inc(s_own, 1)
            pool.wait_ge(s_own, 2)
            pool.affine_select(out=own[:, :], in_=own[:, :], compare_op=ALU.is_ge, fill=0.0,
                               base=R - 1, pattern=[[R, E]], channel_multiplier=-1).then_inc(s_own, 1)
            pool.memset(ident[:, :], 0.0).then_inc(s_ident, 1)
            pool.wait_ge(s_ident, 1)
            pool.affine_select(out=ident[:, :], in_=ident[:, :], compare_op=ALU.not_equal, fill=1.0,
                               base=0, pattern=[[-1, P]], channel_multiplier=1).then_inc(s_ident, 1)
            pool.wait_ge(s_ident, 2)
            pool.wait_ge(ld_par, 16)
            pool.tensor_tensor(w_base_i[:, :], w_base, ident[:, :], ALU.add).then_inc(s_wbi, 1)

            def lo(p):
                pool.wait_ge(s_whi, p + 1)
                pool.tensor_tensor(wlo[:, p, :], raw_piece(p), whi[:, p, :], ALU.subtract).then_inc(s_wlo, 1)

            steps = 0
            G = E // 2
            mask = w3in[:, E:E + 1, :].to_broadcast([P, G, P])
            pool_steps = []
            for g in (0, G):
                pool_steps.append((w3in[:, g:g + G, :], w3in[:, g:g + G, :], mask, ALU.mult))
            for b in range(B):
                for g in (0, G):
                    y = condb[:, b, g:g + G].unsqueeze(2).to_broadcast([P, G, P])
                    pool_steps.append((w3sum[:, g:g + G, :], w3in[:, g:g + G, :], y, ALU.mult))
                n = G
                while n:
                    pool_steps.append((w3sum[:, 0:n, :], w3sum[:, 0:n, :], w3sum[:, n:2 * n, :], ALU.add))
                    n //= 2
                pool_steps.append((w3[:, b, :], w3sum[:, 0, :], ident[:, :], ALU.add))

            for b in range(B):
                pool.wait_ge(s_xlo, b + 1)
                pool.tensor_tensor(x1[:, b, :], xhi[:, 0, b, :], xlo[:, 0, b, :], ALU.add).then_inc(s_x1, 1)
            pool.wait_ge(ld_cond, 16)
            for p in range(L1_BLOCKS, NPIECES):
                lo(p)
                if p == L1_BLOCKS + 1:
                    pool.wait_ge(ld_w3, 16)
                if p > L1_BLOCKS and pool_steps:
                    out, a, c, op = pool_steps.pop(0)
                    if steps:
                        pool.wait_ge(s_f3, steps)
                    pool.tensor_tensor(out, a, c, op).then_inc(s_f3, 1)
                    steps += 1
            assert not pool_steps

        N_F3 = B + B * (2 + 3 + 1)

        @block.scalar
        def _(sc):
            sc.dma_start(condb[:, :, :].rearrange("p b e -> p (b e)"),
                         cond.rearrange("(a b) e -> a (b e)", a=1).to_broadcast([P, B * E])).then_inc(ld_cond, 16)
            sc.wait_ge(s_dif, 1)
            sc.activation(ex[:, :, :], dif[:, :, :], ACT.Exp).then_inc(s_exp, 1)
            sc.wait_ge(s_warm, 1)
            sc.activation(tiny[:, 0:1], warm[:, 0:1], ACT.Gelu_apprx_tanh)

            def hi(p):
                wait_piece_loaded(sc, p)
                sc.activation(whi[:, p, :], raw_piece(p), ACT.Copy).then_inc(s_whi, 1)

            def x_hi(b):
                sc.wait_ge(s_l0, b + 1)
                sc.activation(xhi[:, 0, b, :], acc[b][:, :], ACT.Identity, bias=bias0).then_inc(s_xhi, 1)

            hi(0)
            x_hi(0)
            hi(1)
            x_hi(1)
            hi(2)
            hi(3)

            def h_hi(k):
                sc.wait_ge(s_h, k + 1)
                if k >= HBUFS:
                    sc.wait_ge(s_d, k - HBUFS + 1)
                sc.activation(hhi[:, k % HBUFS, :], h[:, k % HBUFS, :], ACT.Copy).then_inc(s_hhi, 1)

            def x2_hi(b):
                sc.wait_ge(s_x2, b + 1)
                sc.activation(xhi[:, 1, b, :], x2[:, b, :], ACT.Copy).then_inc(s_xhi, 1)

            for k in range(N1):
                sc.wait_ge(s_g, k + 1)
                if k >= 2:
                    sc.wait_ge(s_h, k - 1)
                sc.activation(act[:, k % 2, :], gp[k % PAIRS][:, :], ACT.Gelu_apprx_tanh).then_inc(s_act, 1)
                if k == N1 - 1:
                    sc.activation(tiny[:, 1:2], warm[:, 0:1], ACT.Silu)
                h_hi(k)
                if k >= L1_BLOCKS and k < NPIECES:
                    hi(k)
                if k == 20:
                    x2_hi(0)

            def silu(k):
                b, j = divmod(k - N1, L2_BLOCKS)
                bias = raw_l2[:, b, L2_BLOCKS * PIECE + j:L2_BLOCKS * PIECE + j + 1]
                sc.wait_ge(s_g, k + 1)
                sc.wait_ge(s_h, k - 1)
                sc.activation(act[:, k % 2, :], gp[k % PAIRS][:, :], ACT.Silu, bias=bias).then_inc(s_act, 1)

            silu(N1)
            h_hi(N1)
            x2_hi(1)
            silu(N1 + 1)
            h_hi(N1 + 1)
            silu(N1 + 2)
            h_hi(N1 + 2)
            silu(N1 + 3)
            h_hi(N1 + 3)
            for b in range(B):
                sc.wait_ge(s_l3o, 2 * b + 1)
                sc.activation(res[:, b, :HALF], l3out[b][0], ACT.Identity, bias=bias3).then_inc(s_resa, 1)
                sc.wait_ge(s_resa, b + 1)
                sc.dma_start(out_t[:, b * T:b * T + HALF], res[:, b, :HALF]).then_inc(s_out, 16)

        @block.tensor
        def _(pe):
            pe.wait_ge(s_warm, 1)
            for _ in range(4):
                pe.matmul(acc[1][:, 0:P], warm[:, 0:P], warm[:, 0:P], start=True, stop=True)
            pe.wait_ge(s_bsw, B)
            pe.matmul(fold, a_er, bsw[:, :, :], start=True, stop=True).then_inc(s_fold, 1)
            pe.wait_ge(s_w0, 1)
            for b in range(B):
                pe.wait_ge(ld_x[b], 16)
                pe.matmul(acc[b][:, :], w0[:, b, :], x0[:, b, :], start=True, stop=True).then_inc(s_l0, 1)

            def three(out, w_hi, w_lo, v_hi, v_lo, start, stop):
                pe.matmul(out, w_hi, v_hi, start=start, stop=False)
                pe.matmul(out, w_lo, v_hi, start=False, stop=False)
                return pe.matmul(out, w_hi, v_lo, start=False, stop=stop)

            def gate_up(k):
                p, b, layer = piece_of(k), BLOCK_BATCH[k], int(k >= N1)
                pe.wait_ge(s_whi, p + 1)
                if p < L1_BLOCKS:
                    pe.wait_ge(s_wlo_sh, p + 1)
                else:
                    pe.wait_ge(s_wlo, p - L1_BLOCKS + 1)
                pe.wait_ge(s_xlo, 2 * layer + b + 1)
                if k >= PAIRS:
                    pe.wait_ge(s_h, k - PAIRS + 1)
                elif k == 2:
                    pe.wait_ge(s_w0, 1)
                x_h, x_l = xhi[:, layer, b, :], xlo[:, layer, b, :]
                three(gp[k % PAIRS][:, :], whi[:, p, 0:P], wlo[:, p, 0:P], x_h, x_l, True, True)\
                    .then_inc(s_g, 1)
                three(up[k % PAIRS][:, :], whi[:, p, P:2 * P], wlo[:, p, P:2 * P], x_h, x_l, True, True)\
                    .then_inc(s_u, 1)

            def down(k):
                p, b = piece_of(k), BLOCK_BATCH[k]
                pe.wait_ge(s_hlo, k + 1)
                if k in (0, L1_BLOCKS):
                    pe.wait_ge(s_xlo, b + 1)
                elif is_first(k):
                    pe.wait_ge(s_x2, b + 1)
                i = k % HBUFS
                three(acc[b][:, :], whi[:, p, 2 * P:], wlo[:, p, 2 * P:], hhi[:, i, :], hlo[:, i, :],
                      is_first(k), is_last(k)).then_inc(s_d, 1)

            def layer3(b):
                if b == 0:
                    pe.wait_ge(s_f3, N_F3)
                pe.wait_ge(s_h, N1 + 2 + b)
                for i in range(2):
                    pe.wait_ge(s_x3, 2 * b + i + 1)
                    pe.matmul(l3out[b][i], w3[:, b, :], x3[:, b, i * HALF:(i + 1) * HALF],
                              start=True, stop=True).then_inc(s_l3o, 1)

            for k in range(N1):
                gate_up(k)
                if k >= LAG:
                    down(k - LAG)
            gate_up(N1)
            down(N1 - 2)
            down(N1 - 1)
            gate_up(N1 + 1)
            down(N1)
            gate_up(N1 + 2)
            down(N1 + 1)
            gate_up(N1 + 3)
            down(N1 + 2)
            layer3(0)
            down(N1 + 3)
            layer3(1)

        @block.vector
        def _(ve):
            ve.memset(warm[:, :], 0.0).then_inc(s_warm, 1)
            ve.wait_ge(ld_cond, 16)
            ve.wait_ge(s_own, 3)
            ve.tensor_tensor(picked[:, :, :], condb[:, :, :], own[:, :].unsqueeze(1).to_broadcast([P, B, E]),
                             ALU.mult).then_inc(s_wcol, 1)
            ve.wait_ge(s_wcol, 1)
            ve.tensor_reduce(wcol[:, :], picked[:, :, :], AX.X, ALU.add).then_inc(s_wcol, 1)
            for b in range(B):
                ve.max(top[:, b, :], condb[:, b, :]).then_inc(s_top, 1)
            for b in range(B):
                ve.wait_ge(s_top, b + 1)
                ve.max_index(idx[:, b, :], top[:, b, :], condb[:, b, :]).then_inc(s_idx, 1)
            ve.tensor_tensor(dif[:, :, :], top[:, :, :], top[:, :, 0:1].to_broadcast([P, B, 8]), ALU.subtract)\
              .then_inc(s_dif, 1)
            ve.wait_ge(ld_par, 16)
            ve.wait_ge(s_wcol, 2)
            for b in range(B):
                ve.tensor_scalar(bsw[:, b, :], b_er, wcol[:, b:b + 1], LORA_SCALE, ALU.mult, ALU.mult)\
                  .then_inc(s_bsw, 1)
            ve.wait_ge(s_fold, 1)
            ve.wait_ge(s_wbi, 1)
            ve.tensor_tensor(w0[:, :, :], fold, w_base_i[:, :].unsqueeze(1).to_broadcast([P, B, P]), ALU.add)\
              .then_inc(s_w0, 1)

            def lo(p):
                ve.wait_ge(s_whi, p + 1)
                ve.tensor_tensor(wlo[:, p, :], raw_piece(p), whi[:, p, :], ALU.subtract).then_inc(s_wlo_sh, 1)

            def x_lo(b):
                ve.wait_ge(s_xhi, b + 1)
                ve.scalar_tensor_tensor(out=xlo[:, 0, b, :], in0=acc[b][:, :], scalar=bias0, in1=xhi[:, 0, b, :],
                                        op0=ALU.add, op1=ALU.subtract).then_inc(s_xlo, 1)

            lo(0)
            x_lo(0)
            lo(1)
            x_lo(1)
            lo(2)
            lo(3)

            def hidden(k):
                i = k % HBUFS
                ve.wait_ge(s_act, k + 1)
                ve.wait_ge(s_u, k + 1)
                if k >= HBUFS:
                    ve.wait_ge(s_hhi, k - HBUFS + 1)
                    ve.wait_ge(s_hlo, k - HBUFS + 1)
                a, u = act[:, k % 2, :], up[k % PAIRS][:, :]
                if k >= N1:
                    b, j = divmod(k - N1, L2_BLOCKS)
                    c = L2_BLOCKS * PIECE + L2_BLOCKS + j
                    ve.scalar_tensor_tensor(out=h[:, i, :], in0=u, scalar=raw_l2[:, b, c:c + 1], in1=a,
                                            op0=ALU.add, op1=ALU.mult).then_inc(s_h, 1)
                elif expert_of(k) is None:
                    ve.tensor_tensor(h[:, i, :], u, a, ALU.mult).then_inc(s_h, 1)
                else:
                    b, r = expert_of(k)
                    ve.scalar_tensor_tensor(out=h[:, i, :], in0=u, scalar=gate_w[:, b, r:r + 1], in1=a,
                                            op0=ALU.mult, op1=ALU.mult).then_inc(s_h, 1)

            def h_lo(k):
                i = k % HBUFS
                ve.wait_ge(s_hhi, k + 1)
                if k >= HBUFS:
                    ve.wait_ge(s_d, k - HBUFS + 1)
                ve.tensor_tensor(hlo[:, i, :], h[:, i, :], hhi[:, i, :], ALU.subtract).then_inc(s_hlo, 1)

            def router_weights():
                n = 0

                def done(ins):
                    nonlocal n
                    n += 1
                    ins.then_inc(s_rt, 1)
                    ve.wait_ge(s_rt, n)

                ve.wait_ge(s_exp, 1)
                done(ve.tensor_reduce(ssum[:, :], ex[:, :, :], AX.X, ALU.add))
                done(ve.reciprocal(rsum[:, :], ssum[:, :]))
                done(ve.tensor_tensor(rw[:, :, :], ex[:, :, 0:TOP],
                                      rsum[:, :].unsqueeze(2).to_broadcast([P, B, TOP]), ALU.mult))
                done(ve.tensor_reduce(pair[:, :], rw[:, :, :], AX.X, ALU.add))
                done(ve.reciprocal(rpair[:, :], pair[:, :]))
                done(ve.tensor_tensor(wn[:, :, :], rw[:, :, :],
                                      rpair[:, :].unsqueeze(2).to_broadcast([P, B, TOP]), ALU.mult))
                done(ve.tensor_scalar(wa[:, :, :], wn[:, :, :], W_SCALE, None, ALU.mult))
                done(ve.scalar_tensor_tensor(out=gate_w[:, :, :], in0=wn[:, :, :], scalar=1.0 - W_SCALE,
                                             in1=wa[:, :, :], op0=ALU.mult, op1=ALU.add))

            def x2_sum(b):
                k = N1 - 1 if b else N1 - TOP * L1_BLOCKS - 1
                ve.wait_ge(s_d, k + 1)
                ve.wait_ge(s_x1, b + 1)
                ve.tensor_tensor(x2[:, b, :], acc[b][:, :], x1[:, b, :], ALU.add).then_inc(s_x2, 1)

            def x2_lo(b):
                ve.wait_ge(s_xhi, B + b + 1)
                ve.tensor_tensor(xlo[:, 1, b, :], x2[:, b, :], xhi[:, 1, b, :], ALU.subtract).then_inc(s_xlo, 1)

            def x3_sum(b):
                c = L2_BLOCKS * PIECE + 2 * L2_BLOCKS
                ve.wait_ge(s_d, N1 + L2_BLOCKS * (b + 1))
                for i in range(2):
                    t = slice(i * HALF, (i + 1) * HALF)
                    ve.scalar_tensor_tensor(out=x3[:, b, t], in0=acc[b][:, t], scalar=raw_l2[:, b, c:c + 1],
                                            in1=x2[:, b, t], op0=ALU.add, op1=ALU.add).then_inc(s_x3, 1)

            for k in range(N1):
                hidden(k)
                h_lo(k)
                if k == 1:
                    router_weights()
                if k == 19:
                    x2_sum(0)
                if k == 20:
                    x2_lo(0)
            hidden(N1)
            h_lo(N1)
            x2_sum(1)
            x2_lo(1)
            hidden(N1 + 1)
            h_lo(N1 + 1)
            hidden(N1 + 2)
            h_lo(N1 + 2)
            x3_sum(0)
            hidden(N1 + 3)
            h_lo(N1 + 3)

            def result(b):
                ve.wait_ge(s_l3o, 2 * b + 2)
                ve.tensor_scalar(res[:, b, HALF:], l3out[b][1], bias3, None, ALU.add).then_inc(s_resv, 1)

            result(0)
            x3_sum(1)
            result(1)


def kernel(**inputs):
    import numpy as np
    import concourse.bacc as bacc
    from concourse.bass_utils import run_bass_kernel_spmd

    i = {name: np.asarray(a) for name, a in inputs.items()}

    def gate_up_down(gate, up_, down, blocks):
        lead = gate.shape[:-2]
        g = np.moveaxis(gate.reshape(*lead, P, blocks, P), -2, -3)
        u = np.moveaxis(up_.reshape(*lead, P, blocks, P), -2, -3)
        d = down.reshape(*lead, blocks, P, P)
        return np.concatenate([g, u, d], axis=-1)

    def rows(pieces):
        m = np.moveaxis(pieces, -3, -2)
        return m.reshape(*m.shape[:-2], -1)

    skill = rows(gate_up_down(i["L1_cond_skill_gate"], i["L1_cond_skill_up"], i["L1_cond_skill_down"], L1_BLOCKS))
    shared = gate_up_down(i["L1_cond_shared_gate"], i["L1_cond_shared_up"], i["L1_cond_shared_down"], L1_BLOCKS)
    l2w = rows(gate_up_down(np.swapaxes(i["L2_cond_W_up"], 1, 2), np.swapaxes(i["L2_cond_W_gate"], 1, 2),
                            np.swapaxes(i["L2_cond_W_down"], 1, 2), L2_BLOCKS))
    l2b = [np.swapaxes(i[n].reshape(E, -1, P), 1, 2) for n in ("L2_cond_b_up", "L2_cond_b_gate", "L2_cond_b_down")]
    arrays = {
        "x_t": i["x"].reshape(B * T, P).T,
        "cond": i["cond_8"],
        "l0": np.concatenate([i["L0_cond_As"].reshape(P, P), np.swapaxes(i["L0_cond_Bs"], 1, 2).reshape(P, P),
                              i["L0_cond_W_base"].T, i["L0_cond_b_base"][:, None], i["L3_cond_bias"][:, None]], axis=1),
        "shared": shared,
        "skill": skill,
        "l2": np.concatenate([l2w, *l2b], axis=-1),
        "l3": np.concatenate([np.moveaxis(i["L3_cond_weight"], -1, 0).reshape(P, E * P), i["L3_cond_mask"].T], axis=1),
    }
    arrays = {name: np.ascontiguousarray(a) for name, a in arrays.items()}
    nc = bacc.Bacc("TRN2", target_bir_lowering=False, num_devices=1)
    ins = [nc.dram_tensor(name, a.shape, mybir.dt.from_np(a.dtype), kind="ExternalInput").ap()
           for name, a in arrays.items()]
    out_t = nc.dram_tensor("out_t", (P, B * T), F32, kind="ExternalOutput").ap()
    build(nc, *ins, out_t)
    got = run_bass_kernel_spmd(nc, [arrays], core_ids=[0]).results[0]["out_t"]
    return np.ascontiguousarray(got.T).reshape(B, T, P)
```

```python
from contextlib import ExitStack

import concourse.bass as bass
from concourse import mybir

ALU = mybir.AluOpType
ACT = mybir.ActivationFunctionType
AX = mybir.AxisListType
F32 = mybir.dt.float32
F32R = mybir.dt.float32r
U32 = mybir.dt.uint32

P = 128
B = 2
T = 512
HALF = T // 2
E = 8
TOP = 2
LORA_SCALE = 2.0
W_SCALE = 1.0 / 12

L1_BLOCKS = 4
L2_BLOCKS = 2
PIECE = 3 * P
L2_BIAS = 2 * L2_BLOCKS + 1

BLOCK_BATCH = [0] * L1_BLOCKS + [1] * L1_BLOCKS + [0] * (TOP * L1_BLOCKS) + [1] * (TOP * L1_BLOCKS)
N1 = len(BLOCK_BATCH)
BLOCK_BATCH += [0] * L2_BLOCKS + [1] * L2_BLOCKS
N = len(BLOCK_BATCH)
NPIECES = N - L1_BLOCKS
PAIRS = 3
ROUTER_STEPS = 8
X2_BLOCK = 20
HBUFS = 3
WARM_MATMULS = 7
LAG = 2
POOL_LO = (N - 3, N - 2)


def piece_of(k):
    return k if k < L1_BLOCKS else k - L1_BLOCKS


def is_first(k):
    return k in (0, L1_BLOCKS) or (k >= N1 and (k - N1) % L2_BLOCKS == 0)


def is_last(k):
    return k in (N1 - TOP * L1_BLOCKS - 1, N1 - 1) or (k >= N1 and (k - N1) % L2_BLOCKS == L2_BLOCKS - 1)


def expert_of(k):
    if 2 * L1_BLOCKS <= k < N1:
        n = (k - 2 * L1_BLOCKS) // L1_BLOCKS
        return n // TOP, n % TOP
    return None


def build(nc, x_t, cond, l0, shared, skill, l2, l3, out_t):
    ctx = ExitStack()
    with ctx:
        def sb(name, shape, dt=F32):
            return ctx.enter_context(nc.sbuf_tensor(name, shape, dt))

        def sem(name):
            return ctx.enter_context(nc.semaphore(name))

        x0 = sb("x0", [P, B, T])
        condb = sb("condb", [P, B, E])
        own = sb("own", [P, E])
        picked = sb("picked", [P, B, E])
        wcol = sb("wcol", [P, B])
        params = sb("params", [P, 3 * P + 2])
        a_er, b_er, w_base = params[:, 0:P], params[:, P:2 * P], params[:, 2 * P:3 * P]
        bias0, bias3 = params[:, 3 * P:3 * P + 1], params[:, 3 * P + 1:3 * P + 2]
        bsw = sb("bsw", [P, B, P])
        w_base_i = sb("w_base_i", [P, P])
        w0 = sb("w0", [P, B, P])
        ident = sb("ident", [P, P])
        x1 = sb("x1", [P, B, T])
        x2 = sb("x2", [P, B, T])
        x3 = sb("x3", [P, B, T])
        xhi = sb("xhi", [P, 2, B, T], F32R)
        xlo = sb("xlo", [P, 2, B, T], F32R)
        act = sb("act", [P, 2, T])
        h = sb("h", [P, HBUFS, T])
        hhi = sb("hhi", [P, HBUFS, T], F32R)
        hlo = sb("hlo", [P, HBUFS, T], F32R)
        raw_shared = sb("raw_shared", [P, L1_BLOCKS, PIECE])
        raw_skill = sb("raw_skill", [P, B * TOP, L1_BLOCKS * PIECE])
        raw_l2 = sb("raw_l2", [P, B, L2_BLOCKS * PIECE + L2_BIAS])
        whi = sb("whi", [P, NPIECES, PIECE], F32R)
        wlo = sb("wlo", [P, NPIECES, PIECE], F32R)
        w3in = sb("w3in", [P, E + 1, P])
        w3sum = sb("w3sum", [P, E, P])
        w3 = sb("w3", [P, B, P])
        res = sb("res", [P, B, T])
        warm = sb("warm", [P, P])
        tiny = sb("tiny", [P, 2])
        top = sb("top", [P, B, 8])
        idx = sb("idx", [P, B, 8], U32)
        dif = sb("dif", [P, B, 8])
        ex = sb("ex", [P, B, 8])
        ssum = sb("ssum", [P, B])
        rsum = sb("rsum", [P, B])
        rw = sb("rw", [P, B, TOP])
        pair = sb("pair", [P, B])
        rpair = sb("rpair", [P, B])
        wn = sb("wn", [P, B, TOP])
        wa = sb("wa", [P, B, TOP])
        gate_w = sb("gate_w", [P, B, TOP])

        gp = [ctx.enter_context(nc.psum_tensor(f"gp{i}", [P, T], F32)) for i in range(PAIRS)]
        up = [ctx.enter_context(nc.psum_tensor(f"up{i}", [P, T], F32)) for i in range(PAIRS)]
        acc = [ctx.enter_context(nc.psum_tensor(f"acc{i}", [P, T], F32)) for i in range(B)]
        fold = [gp[1][:, :P], up[1][:, :P]]
        l0out = [[acc[0][:, :HALF], acc[1][:, :HALF]], [gp[2][:, :HALF], up[2][:, :HALF]]]
        y1 = [acc[1][:, :HALF], up[1][:, :HALF]]
        l3out0 = gp[1][:, :]
        l3out1 = [gp[2][:, :HALF], up[2][:, :HALF]]

        ld_cond, ld_par, ld_w3 = sem("ld_cond"), sem("ld_par"), sem("ld_w3")
        ld_x = [sem(f"ld_x{b}") for b in range(B)]
        ld_sh = [sem(f"ld_sh{i}") for i in range(L1_BLOCKS)]
        ld_sk = [sem(f"ld_sk{i}") for i in range(B * TOP)]
        ld_l2 = [sem(f"ld_l2{b}") for b in range(B)]
        s_warm = sem("s_warm")
        s_ident = sem("s_ident")
        s_own = sem("s_own")
        s_wcol = sem("s_wcol")
        s_wbi = sem("s_wbi")
        s_top = sem("s_top")
        s_idx = sem("s_idx")
        s_dif = sem("s_dif")
        s_exp = sem("s_exp")
        s_rt = sem("s_rt")
        s_bsw = sem("s_bsw")
        s_fold = sem("s_fold")
        s_w0 = sem("s_w0")
        s_l0 = sem("s_l0")
        s_x1hi = sem("s_x1hi")
        s_x1lo = sem("s_x1lo")
        s_x1 = sem("s_x1")
        s_x2 = sem("s_x2")
        s_x2hi = sem("s_x2hi")
        s_x2lo = sem("s_x2lo")
        s_x3 = sem("s_x3")
        s_whi = sem("s_whi")
        s_wlo0 = sem("s_wlo0")
        s_wlo = sem("s_wlo")
        s_g = sem("s_g")
        s_u = sem("s_u")
        s_d = sem("s_d")
        s_act = sem("s_act")
        s_h = sem("s_h")
        s_hhi = sem("s_hhi")
        s_hlo = sem("s_hlo")
        s_hlop = sem("s_hlop")
        s_f3 = sem("s_f3")
        s_l3o = sem("s_l3o")
        s_res0 = sem("s_res0")
        s_res1 = [sem(f"s_res1{i}") for i in range(2)]
        s_out = sem("s_out")

        def raw_piece(p):
            if p < L1_BLOCKS:
                return raw_shared[:, p, :]
            q = p - L1_BLOCKS
            if q < B * TOP * L1_BLOCKS:
                i = q % L1_BLOCKS
                return raw_skill[:, q // L1_BLOCKS, i * PIECE:(i + 1) * PIECE]
            q -= B * TOP * L1_BLOCKS
            i = q % L2_BLOCKS
            return raw_l2[:, q // L2_BLOCKS, i * PIECE:(i + 1) * PIECE]

        def hlo_count(k):
            return k + 1 - sum(q <= k for q in POOL_LO)

        def wait_piece_loaded(eng, p):
            if p < L1_BLOCKS:
                eng.wait_ge(ld_sh[p], 16)
            elif p < L1_BLOCKS * (1 + B * TOP):
                eng.wait_ge(ld_sk[p // L1_BLOCKS - 1], 16)
            else:
                eng.wait_ge(ld_l2[(p - L1_BLOCKS * (1 + B * TOP)) // L2_BLOCKS], 16)

        block = ctx.enter_context(nc.Block())

        @block.sync
        def _(sp):
            sp.dma_start(condb[:, :, :].rearrange("p b e -> p (b e)"),
                         cond.rearrange("(a b) e -> a (b e)", a=1).to_broadcast([P, B * E])).then_inc(ld_cond, 16)
            sp.dma_start(params[:, :], l0[:, :]).then_inc(ld_par, 16)
            sp.dma_start(x0[:, 0, :], x_t[:, 0:T]).then_inc(ld_x[0], 16)
            sp.dma_start(raw_shared[:, 0, :], shared[0]).then_inc(ld_sh[0], 16)
            sp.dma_start(x0[:, 1, :], x_t[:, T:2 * T]).then_inc(ld_x[1], 16)
            for i in range(1, L1_BLOCKS):
                sp.dma_start(raw_shared[:, i, :], shared[i]).then_inc(ld_sh[i], 16)
            sp.wait_ge(s_idx, B)
            for b in range(B):
                for r in range(TOP):
                    e = sp.value_load(idx[0:1, b, r:r + 1], min_val=0, max_val=E - 1)
                    n = b * TOP + r
                    sp.dma_start(raw_skill[:, n, :], skill[bass.ds(e, 1), :, :]).then_inc(ld_sk[n], 16)
                    if n == 0:
                        sp.dma_start(w3in[:, :, :], l3.rearrange("p (g o) -> p g o", o=P)).then_inc(ld_w3, 16)
            for b in range(B):
                e = sp.value_load(idx[0:1, b, 0:1], min_val=0, max_val=E - 1)
                sp.dma_start(raw_l2[:, b, :], l2[bass.ds(e, 1), :, :]).then_inc(ld_l2[b], 16)
            sp.wait_ge(s_res1[1], 1)
            sp.dma_start(out_t[:, T + HALF:], res[:, 1, HALF:]).then_inc(s_out, 16)
            sp.wait_ge(s_out, 16 * 3)

        @block.gpsimd
        def _(pool):
            R = P // E
            pool.memset(own[:, :], 1.0).then_inc(s_own, 1)
            pool.wait_ge(s_own, 1)
            pool.affine_select(out=own[:, :], in_=own[:, :], compare_op=ALU.is_ge, fill=0.0,
                               base=0, pattern=[[-R, E]], channel_multiplier=1).then_inc(s_own, 1)
            pool.wait_ge(s_own, 2)
            pool.affine_select(out=own[:, :], in_=own[:, :], compare_op=ALU.is_ge, fill=0.0,
                               base=R - 1, pattern=[[R, E]], channel_multiplier=-1).then_inc(s_own, 1)
            pool.memset(ident[:, :], 0.0).then_inc(s_ident, 1)
            pool.wait_ge(s_ident, 1)
            pool.affine_select(out=ident[:, :], in_=ident[:, :], compare_op=ALU.not_equal, fill=1.0,
                               base=0, pattern=[[-1, P]], channel_multiplier=1).then_inc(s_ident, 1)
            pool.wait_ge(s_ident, 2)
            pool.wait_ge(ld_par, 16)
            pool.tensor_tensor(w_base_i[:, :], w_base, ident[:, :], ALU.add).then_inc(s_wbi, 1)

            def lo(p):
                pool.wait_ge(s_whi, p + 1)
                pool.tensor_tensor(wlo[:, p, :], raw_piece(p), whi[:, p, :], ALU.subtract).then_inc(s_wlo, 1)

            steps = 0
            G = E // 2
            mask = w3in[:, E:E + 1, :].to_broadcast([P, G, P])
            pool_steps = []
            for g in (0, G):
                pool_steps.append((w3in[:, g:g + G, :], w3in[:, g:g + G, :], mask, ALU.mult))
            for b in range(B):
                for g in (0, G):
                    y = condb[:, b, g:g + G].unsqueeze(2).to_broadcast([P, G, P])
                    pool_steps.append((w3sum[:, g:g + G, :], w3in[:, g:g + G, :], y, ALU.mult))
                n = G
                while n:
                    pool_steps.append((w3sum[:, 0:n, :], w3sum[:, 0:n, :], w3sum[:, n:2 * n, :], ALU.add))
                    n //= 2
                pool_steps.append((w3[:, b, :], w3sum[:, 0, :], ident[:, :], ALU.add))

            for p in range(1, L1_BLOCKS):
                lo(p)
            for b in range(B):
                pool.wait_ge(s_x1lo, 2 * (b + 1))
                pool.tensor_tensor(x1[:, b, :], xhi[:, 0, b, :], xlo[:, 0, b, :], ALU.add).then_inc(s_x1, 1)
            pool.wait_ge(ld_cond, 16)
            for p in range(L1_BLOCKS, NPIECES):
                lo(p)
                if p == L1_BLOCKS + 1:
                    pool.wait_ge(ld_w3, 16)
                if p > L1_BLOCKS and pool_steps:
                    out, a, c, op = pool_steps.pop(0)
                    if steps:
                        pool.wait_ge(s_f3, steps)
                    pool.tensor_tensor(out, a, c, op).then_inc(s_f3, 1)
                    steps += 1
            assert not pool_steps
            for k in POOL_LO:
                i = k % HBUFS
                pool.wait_ge(s_hhi, k + 1)
                pool.wait_ge(s_d, k - HBUFS + 1)
                pool.tensor_tensor(hlo[:, i, :], h[:, i, :], hhi[:, i, :], ALU.subtract).then_inc(s_hlop, 1)

        N_F3 = 2 + B * (2 + 3 + 1)

        @block.scalar
        def _(sc):
            sc.wait_ge(s_dif, 1)
            sc.activation(ex[:, :, :], dif[:, :, :], ACT.Exp).then_inc(s_exp, 1)
            sc.wait_ge(s_warm, 1)
            sc.activation(tiny[:, 0:1], warm[:, 0:1], ACT.Gelu_apprx_tanh)

            def hi(p):
                wait_piece_loaded(sc, p)
                sc.activation(whi[:, p, :], raw_piece(p), ACT.Copy).then_inc(s_whi, 1)

            def x1_hi(b):
                for i in range(2):
                    sc.wait_ge(s_l0, 2 * b + i + 1)
                    sc.activation(xhi[:, 0, b, i * HALF:(i + 1) * HALF], l0out[b][i], ACT.Identity, bias=bias0)\
                        .then_inc(s_x1hi, 1)

            hi(0)
            x1_hi(0)
            hi(1)
            x1_hi(1)
            hi(2)
            hi(3)

            def h_hi(k, t=slice(0, T)):
                sc.wait_ge(s_h, k + 1 + (t.start > 0))
                if k >= HBUFS:
                    sc.wait_ge(s_d, k - HBUFS + 1)
                i = k % HBUFS
                sc.activation(hhi[:, i, t], h[:, i, t], ACT.Copy).then_inc(s_hhi, 1)

            def x2_hi(b):
                sc.wait_ge(s_x2, b + 1)
                sc.activation(xhi[:, 1, b, :], x2[:, b, :], ACT.Copy).then_inc(s_x2hi, 1)

            def wait_act(k):
                sc.wait_ge(s_g, k + 1)
                if k >= 2:
                    sc.wait_ge(s_h, k - 1)

            def gelu(k):
                wait_act(k)
                sc.activation(act[:, k % 2, :], gp[k % PAIRS][:, :], ACT.Gelu_apprx_tanh).then_inc(s_act, 1)

            def silu(k):
                b, j = divmod(k - N1, L2_BLOCKS)
                bias = raw_l2[:, b, L2_BLOCKS * PIECE + j:L2_BLOCKS * PIECE + j + 1]
                wait_act(k)
                sc.activation(act[:, k % 2, :], gp[k % PAIRS][:, :], ACT.Silu, bias=bias).then_inc(s_act, 1)

            for k in range(N1 - 1):
                gelu(k)
                if k:
                    h_hi(k - 1)
                if k + 1 >= L1_BLOCKS:
                    hi(k + 1)
                if k == X2_BLOCK:
                    x2_hi(0)
            h_hi(N1 - 2)
            gelu(N1 - 1)
            sc.activation(tiny[:, 1:2], warm[:, 0:1], ACT.Silu)
            h_hi(N1 - 1)
            silu(N1)
            h_hi(N1)
            x2_hi(1)
            silu(N1 + 1)
            h_hi(N1 + 1)
            silu(N1 + 2)
            h_hi(N1 + 2)
            silu(N1 + 3)
            for i in range(2):
                h_hi(N1 + 3, slice(i * HALF, (i + 1) * HALF))
            sc.wait_ge(s_l3o, 1)
            sc.activation(res[:, 0, :], l3out0, ACT.Identity, bias=bias3).then_inc(s_res0, 1)
            sc.wait_ge(s_res0, 1)
            sc.dma_start(out_t[:, 0:T], res[:, 0, :]).then_inc(s_out, 16)
            sc.wait_ge(s_l3o, 2)
            sc.activation(res[:, 1, :HALF], l3out1[0], ACT.Identity, bias=bias3).then_inc(s_res1[0], 1)
            sc.wait_ge(s_res1[0], 1)
            sc.dma_start(out_t[:, T:T + HALF], res[:, 1, :HALF]).then_inc(s_out, 16)

        @block.tensor
        def _(pe):
            def spin(n):
                for _ in range(n):
                    pe.matmul(up[0][:, 0:P], warm[:, :], warm[:, :], start=True, stop=True)

            pe.wait_ge(s_warm, 1)
            spin(WARM_MATMULS)
            for b in range(B):
                pe.wait_ge(s_bsw, b + 1)
                pe.matmul(fold[b], a_er, bsw[:, b, :], start=True, stop=True).then_inc(s_fold, 1)
            spin(1)
            for b in range(B):
                pe.wait_ge(s_w0, b + 1)
                pe.wait_ge(ld_x[b], 16)
                for i in range(2):
                    pe.matmul(l0out[b][i], w0[:, b, :], x0[:, b, i * HALF:(i + 1) * HALF],
                              start=True, stop=True).then_inc(s_l0, 1)

            def hi_passes(out, w_hi, w_lo, v_hi, start):
                pe.matmul(out, w_hi, v_hi, start=start, stop=False)
                return pe.matmul(out, w_lo, v_hi, start=False, stop=False)

            def lo_pass(out, w_hi, v_lo, stop):
                return pe.matmul(out, w_hi, v_lo, start=False, stop=stop)

            def gate_up(k, fresh_input=False):
                p, b, layer = piece_of(k), BLOCK_BATCH[k], int(k >= N1)
                pe.wait_ge(s_whi, p + 1)
                if p == 0:
                    pe.wait_ge(s_wlo0, 1)
                else:
                    pe.wait_ge(s_wlo, p)
                if layer == 0:
                    pe.wait_ge(s_x1hi, 2 * (b + 1))
                else:
                    pe.wait_ge(s_x2hi, b + 1)
                if k >= PAIRS:
                    pe.wait_ge(s_h, k - PAIRS + 1)
                elif k == PAIRS - 1:
                    pe.wait_ge(s_x1lo, 2 * B)
                x_h, x_l = xhi[:, layer, b, :], xlo[:, layer, b, :]
                g, u = gp[k % PAIRS][:, :], up[k % PAIRS][:, :]
                w_g, w_u = (whi[:, p, 0:P], wlo[:, p, 0:P]), (whi[:, p, P:2 * P], wlo[:, p, P:2 * P])

                def wait_lo():
                    if layer == 0:
                        pe.wait_ge(s_x1lo, 2 * (b + 1))
                    else:
                        pe.wait_ge(s_x2lo, b + 1)

                hi_passes(g, *w_g, x_h, True)
                if fresh_input:
                    hi_passes(u, *w_u, x_h, True)
                    wait_lo()
                    lo_pass(g, w_g[0], x_l, True).then_inc(s_g, 1)
                else:
                    wait_lo()
                    lo_pass(g, w_g[0], x_l, True).then_inc(s_g, 1)
                    hi_passes(u, *w_u, x_h, True)
                lo_pass(u, w_u[0], x_l, True).then_inc(s_u, 1)

            def wait_down(k):
                if k in (0, L1_BLOCKS):
                    pe.wait_ge(s_x1lo, 2)
                elif is_first(k):
                    pe.wait_ge(s_x2, BLOCK_BATCH[k] + 1)
                pe.wait_ge(s_hhi, k + 1)

            def wait_down_lo(k):
                if k in POOL_LO:
                    pe.wait_ge(s_hlop, POOL_LO.index(k) + 1)
                else:
                    pe.wait_ge(s_hlo, hlo_count(k))

            def down(k):
                p, i, out = piece_of(k), k % HBUFS, acc[BLOCK_BATCH[k]][:, :]
                wait_down(k)
                hi_passes(out, whi[:, p, 2 * P:], wlo[:, p, 2 * P:], hhi[:, i, :], is_first(k))
                wait_down_lo(k)
                lo_pass(out, whi[:, p, 2 * P:], hlo[:, i, :], is_last(k)).then_inc(s_d, 1)

            def down_by_halves(k):
                p, i = piece_of(k), k % HBUFS
                wait_down(k)
                if is_first(k):
                    pe.wait_ge(s_h, N1 + 2)
                for n in range(2):
                    t = slice(n * HALF, (n + 1) * HALF)
                    if k == N - 1:
                        pe.wait_ge(s_hhi, k + 1 + n)
                    hi_passes(y1[n], whi[:, p, 2 * P:], wlo[:, p, 2 * P:], hhi[:, i, t], is_first(k))
                    if k == N - 1:
                        pe.wait_ge(s_hlo, hlo_count(k) + n)
                    else:
                        wait_down_lo(k)
                    mm = lo_pass(y1[n], whi[:, p, 2 * P:], hlo[:, i, t], is_last(k))
                    if n or k == N - 1:
                        mm.then_inc(s_d, 1)

            for k in range(N1):
                gate_up(k, fresh_input=(k == 0))
                if k >= LAG:
                    down(k - LAG)
            gate_up(N1)
            down(N1 - 2)
            down(N1 - 1)
            gate_up(N1 + 1)
            down(N1)
            gate_up(N1 + 2, fresh_input=True)
            gate_up(N1 + 3)
            down(N1 + 1)
            down_by_halves(N1 + 2)
            pe.wait_ge(s_f3, N_F3)
            pe.wait_ge(s_x3, 1)
            pe.matmul(l3out0, w3[:, 0, :], x3[:, 0, :], start=True, stop=True).then_inc(s_l3o, 1)
            down_by_halves(N1 + 3)
            for n in range(2):
                pe.wait_ge(s_x3, 2 + n)
                pe.matmul(l3out1[n], w3[:, 1, :], x3[:, 1, n * HALF:(n + 1) * HALF],
                          start=True, stop=True).then_inc(s_l3o, 1)

        @block.vector
        def _(ve):
            ve.memset(warm[:, :], 0.0).then_inc(s_warm, 1)
            ve.wait_ge(ld_cond, 16)
            ve.wait_ge(s_own, 3)
            ve.tensor_tensor(picked[:, :, :], condb[:, :, :], own[:, :].unsqueeze(1).to_broadcast([P, B, E]),
                             ALU.mult).then_inc(s_wcol, 1)
            ve.wait_ge(s_wcol, 1)
            ve.tensor_reduce(wcol[:, :], picked[:, :, :], AX.X, ALU.add).then_inc(s_wcol, 1)
            for b in range(B):
                ve.max(top[:, b, :], condb[:, b, :]).then_inc(s_top, 1)
            for b in range(B):
                ve.wait_ge(s_top, b + 1)
                ve.max_index(idx[:, b, :], top[:, b, :], condb[:, b, :]).then_inc(s_idx, 1)
            ve.wait_ge(ld_par, 16)
            for b in range(B):
                ve.wait_ge(s_wcol, 2)
                ve.tensor_scalar(bsw[:, b, :], b_er, wcol[:, b:b + 1], LORA_SCALE, ALU.mult, ALU.mult)\
                  .then_inc(s_bsw, 1)
            ve.tensor_tensor(dif[:, :, :], top[:, :, :], top[:, :, 0:1].to_broadcast([P, B, 8]), ALU.subtract)\
              .then_inc(s_dif, 1)
            for b in range(B):
                ve.wait_ge(s_fold, b + 1)
                ve.wait_ge(s_wbi, 1)
                ve.tensor_tensor(w0[:, b, :], fold[b], w_base_i[:, :], ALU.add).then_inc(s_w0, 1)
            ve.wait_ge(s_whi, 1)
            ve.tensor_tensor(wlo[:, 0, :], raw_piece(0), whi[:, 0, :], ALU.subtract).then_inc(s_wlo0, 1)
            for b in range(B):
                for i in range(2):
                    t = slice(i * HALF, (i + 1) * HALF)
                    ve.wait_ge(s_x1hi, 2 * b + i + 1)
                    ve.scalar_tensor_tensor(out=xlo[:, 0, b, t], in0=l0out[b][i], scalar=bias0, in1=xhi[:, 0, b, t],
                                            op0=ALU.add, op1=ALU.subtract).then_inc(s_x1lo, 1)

            def hidden(k, t=slice(0, T)):
                i = k % HBUFS
                ve.wait_ge(s_act, k + 1)
                ve.wait_ge(s_u, k + 1)
                if k >= HBUFS:
                    ve.wait_ge(s_hhi, k - HBUFS + 1)
                    ve.wait_ge(s_hlo, hlo_count(k - HBUFS))
                a, u = act[:, k % 2, t], up[k % PAIRS][:, t]
                if k >= N1:
                    b, j = divmod(k - N1, L2_BLOCKS)
                    c = L2_BLOCKS * PIECE + L2_BLOCKS + j
                    ve.scalar_tensor_tensor(out=h[:, i, t], in0=u, scalar=raw_l2[:, b, c:c + 1], in1=a,
                                            op0=ALU.add, op1=ALU.mult).then_inc(s_h, 1)
                elif expert_of(k) is None:
                    ve.tensor_tensor(h[:, i, t], u, a, ALU.mult).then_inc(s_h, 1)
                else:
                    b, r = expert_of(k)
                    ve.wait_ge(s_rt, ROUTER_STEPS)
                    ve.scalar_tensor_tensor(out=h[:, i, t], in0=u, scalar=gate_w[:, b, r:r + 1], in1=a,
                                            op0=ALU.mult, op1=ALU.mult).then_inc(s_h, 1)

            def h_lo(k, t=slice(0, T)):
                i = k % HBUFS
                ve.wait_ge(s_hhi, k + 1 + (t.start > 0))
                if k >= HBUFS:
                    ve.wait_ge(s_d, k - HBUFS + 1)
                ve.tensor_tensor(hlo[:, i, t], h[:, i, t], hhi[:, i, t], ALU.subtract).then_inc(s_hlo, 1)

            def router_weights():
                ve.wait_ge(s_exp, 1)
                yield ve.tensor_reduce(ssum[:, :], ex[:, :, :], AX.X, ALU.add)
                yield ve.reciprocal(rsum[:, :], ssum[:, :])
                yield ve.tensor_tensor(rw[:, :, :], ex[:, :, 0:TOP],
                                       rsum[:, :].unsqueeze(2).to_broadcast([P, B, TOP]), ALU.mult)
                yield ve.tensor_reduce(pair[:, :], rw[:, :, :], AX.X, ALU.add)
                yield ve.reciprocal(rpair[:, :], pair[:, :])
                yield ve.tensor_tensor(wn[:, :, :], rw[:, :, :],
                                       rpair[:, :].unsqueeze(2).to_broadcast([P, B, TOP]), ALU.mult)
                yield ve.tensor_scalar(wa[:, :, :], wn[:, :, :], W_SCALE, None, ALU.mult)
                yield ve.scalar_tensor_tensor(out=gate_w[:, :, :], in0=wn[:, :, :], scalar=1.0 - W_SCALE,
                                              in1=wa[:, :, :], op0=ALU.mult, op1=ALU.add)

            def x2_sum(b):
                k = N1 - 1 if b else N1 - TOP * L1_BLOCKS - 1
                ve.wait_ge(s_d, k + 1)
                ve.wait_ge(s_x1, b + 1)
                ve.tensor_tensor(x2[:, b, :], acc[b][:, :], x1[:, b, :], ALU.add).then_inc(s_x2, 1)

            def x2_lo(b):
                ve.wait_ge(s_x2hi, b + 1)
                ve.tensor_tensor(xlo[:, 1, b, :], x2[:, b, :], xhi[:, 1, b, :], ALU.subtract).then_inc(s_x2lo, 1)

            def x3_sum(b, y, t):
                c = L2_BLOCKS * PIECE + 2 * L2_BLOCKS
                ve.scalar_tensor_tensor(out=x3[:, b, t], in0=y, scalar=raw_l2[:, b, c:c + 1],
                                        in1=x2[:, b, t], op0=ALU.add, op1=ALU.add).then_inc(s_x3, 1)

            steps = router_weights()
            for k in range(N1):
                hidden(k)
                if k:
                    h_lo(k - 1)
                if k < ROUTER_STEPS:
                    if k:
                        ve.wait_ge(s_rt, k)
                    next(steps).then_inc(s_rt, 1)
                if k == X2_BLOCK - 1:
                    x2_sum(0)
                if k == X2_BLOCK + 1:
                    x2_lo(0)
            h_lo(N1 - 1)
            hidden(N1)
            x2_sum(1)
            h_lo(N1)
            x2_lo(1)
            hidden(N1 + 1)
            hidden(N1 + 2)
            halves = [slice(i * HALF, (i + 1) * HALF) for i in range(2)]
            for t in halves:
                hidden(N1 + 3, t)
            ve.wait_ge(s_d, N1 + 2)
            x3_sum(0, acc[0][:, :], slice(0, T))
            for t in halves:
                h_lo(N1 + 3, t)
            for n, t in enumerate(halves):
                ve.wait_ge(s_d, N + n)
                x3_sum(1, y1[n], t)
            ve.wait_ge(s_l3o, 3)
            ve.tensor_scalar(res[:, 1, HALF:], l3out1[1], bias3, None, ALU.add).then_inc(s_res1[1], 1)


def kernel(**inputs):
    import numpy as np
    import concourse.bacc as bacc
    from concourse.bass_utils import run_bass_kernel_spmd

    i = {name: np.asarray(a) for name, a in inputs.items()}

    def gate_up_down(gate, up_, down, blocks):
        lead = gate.shape[:-2]
        g = np.moveaxis(gate.reshape(*lead, P, blocks, P), -2, -3)
        u = np.moveaxis(up_.reshape(*lead, P, blocks, P), -2, -3)
        d = down.reshape(*lead, blocks, P, P)
        return np.concatenate([g, u, d], axis=-1)

    def rows(pieces):
        m = np.moveaxis(pieces, -3, -2)
        return m.reshape(*m.shape[:-2], -1)

    skill = rows(gate_up_down(i["L1_cond_skill_gate"], i["L1_cond_skill_up"], i["L1_cond_skill_down"], L1_BLOCKS))
    shared = gate_up_down(i["L1_cond_shared_gate"], i["L1_cond_shared_up"], i["L1_cond_shared_down"], L1_BLOCKS)
    l2w = rows(gate_up_down(np.swapaxes(i["L2_cond_W_up"], 1, 2), np.swapaxes(i["L2_cond_W_gate"], 1, 2),
                            np.swapaxes(i["L2_cond_W_down"], 1, 2), L2_BLOCKS))
    l2b = [np.swapaxes(i[n].reshape(E, -1, P), 1, 2) for n in ("L2_cond_b_up", "L2_cond_b_gate", "L2_cond_b_down")]
    arrays = {
        "x_t": i["x"].reshape(B * T, P).T,
        "cond": i["cond_8"],
        "l0": np.concatenate([i["L0_cond_As"].reshape(P, P), np.swapaxes(i["L0_cond_Bs"], 1, 2).reshape(P, P),
                              i["L0_cond_W_base"].T, i["L0_cond_b_base"][:, None], i["L3_cond_bias"][:, None]], axis=1),
        "shared": shared,
        "skill": skill,
        "l2": np.concatenate([l2w, *l2b], axis=-1),
        "l3": np.concatenate([np.moveaxis(i["L3_cond_weight"], -1, 0).reshape(P, E * P), i["L3_cond_mask"].T], axis=1),
    }
    arrays = {name: np.ascontiguousarray(a) for name, a in arrays.items()}
    nc = bacc.Bacc("TRN2", target_bir_lowering=False, num_devices=1)
    ins = [nc.dram_tensor(name, a.shape, mybir.dt.from_np(a.dtype), kind="ExternalInput").ap()
           for name, a in arrays.items()]
    out_t = nc.dram_tensor("out_t", (P, B * T), F32, kind="ExternalOutput").ap()
    build(nc, *ins, out_t)
    got = run_bass_kernel_spmd(nc, [arrays], core_ids=[0]).results[0]["out_t"]
    return np.ascontiguousarray(got.T).reshape(B, T, P)
```

```python
from contextlib import ExitStack

import concourse.bass as bass
from concourse import mybir

ALU = mybir.AluOpType
ACT = mybir.ActivationFunctionType
AX = mybir.AxisListType
F32 = mybir.dt.float32
F32R = mybir.dt.float32r
U32 = mybir.dt.uint32

P = 128
B = 2
T = 512
HALF = T // 2
E = 8
TOP = 2
LORA_SCALE = 2.0
W_SCALE = 1.0 / 12

L1_BLOCKS = 4
L2_BLOCKS = 2
PIECE = 3 * P
L2_BIAS = 2 * L2_BLOCKS + 1

BLOCK_BATCH = [0] * L1_BLOCKS + [1] * L1_BLOCKS + [0] * (TOP * L1_BLOCKS) + [1] * (TOP * L1_BLOCKS)
N1 = len(BLOCK_BATCH)
BLOCK_BATCH += [0] * L2_BLOCKS + [1] * L2_BLOCKS
N = len(BLOCK_BATCH)
NPIECES = N - L1_BLOCKS
DVE_LO = 2
PAIRS = 3
ROUTER_STEPS = 8
L3_STEPS = 2 + B * (2 + 3 + 1)
X2_BLOCK = 20
HBUFS = 3
WARM_MATMULS = 24
LAG = 2


def piece_of(k):
    return k if k < L1_BLOCKS else k - L1_BLOCKS


def is_first(k):
    return k in (0, L1_BLOCKS) or (k >= N1 and (k - N1) % L2_BLOCKS == 0)


def is_last(k):
    return k in (N1 - TOP * L1_BLOCKS - 1, N1 - 1) or (k >= N1 and (k - N1) % L2_BLOCKS == L2_BLOCKS - 1)


def expert_of(k):
    if 2 * L1_BLOCKS <= k < N1:
        n = (k - 2 * L1_BLOCKS) // L1_BLOCKS
        return n // TOP, n % TOP
    return None


def build(nc, x_t, cond, l0, shared, skill, l2, l3, out_t):
    ctx = ExitStack()
    with ctx:
        def sb(name, shape, dt=F32):
            return ctx.enter_context(nc.sbuf_tensor(name, shape, dt))

        def sem(name):
            return ctx.enter_context(nc.semaphore(name))

        x0 = sb("x0", [P, B, T])
        condb = sb("condb", [P, B, E])
        own = sb("own", [P, E])
        picked = sb("picked", [P, B, E])
        wcol = sb("wcol", [P, B])
        params = sb("params", [P, 3 * P + 2])
        a_er, b_er, w_base = params[:, 0:P], params[:, P:2 * P], params[:, 2 * P:3 * P]
        bias0, bias3 = params[:, 3 * P:3 * P + 1], params[:, 3 * P + 1:3 * P + 2]
        bsw = sb("bsw", [P, B, P])
        w_base_i = sb("w_base_i", [P, P])
        w0 = sb("w0", [P, B, P])
        ident = sb("ident", [P, P])
        x1 = sb("x1", [P, B, T])
        x2 = sb("x2", [P, B, T])
        x3 = sb("x3", [P, B, T])
        xhi = sb("xhi", [P, 2, B, T], F32R)
        xlo = sb("xlo", [P, 2, B, T], F32R)
        act = sb("act", [P, 2, T])
        h = sb("h", [P, HBUFS, T])
        hhi = sb("hhi", [P, HBUFS, T], F32R)
        hlo = sb("hlo", [P, HBUFS, T], F32R)
        raw_shared = sb("raw_shared", [P, L1_BLOCKS, PIECE])
        raw_skill = sb("raw_skill", [P, B * TOP, L1_BLOCKS * PIECE])
        raw_l2 = sb("raw_l2", [P, B, L2_BLOCKS * PIECE + L2_BIAS])
        whi = sb("whi", [P, NPIECES, PIECE], F32R)
        wlo = sb("wlo", [P, NPIECES, PIECE], F32R)
        w3in = sb("w3in", [P, E + 1, P])
        w3sum = sb("w3sum", [P, E, P])
        w3 = sb("w3", [P, B, P])
        res = sb("res", [P, B, T])
        warm = sb("warm", [P, P], mybir.dt.bfloat16)
        tiny = sb("tiny", [P, 2])
        top = sb("top", [P, B, 8])
        idx = sb("idx", [P, B, 8], U32)
        dif = sb("dif", [P, B, 8])
        ex = sb("ex", [P, B, 8])
        ssum = sb("ssum", [P, B])
        rsum = sb("rsum", [P, B])
        rw = sb("rw", [P, B, TOP])
        pair = sb("pair", [P, B])
        rpair = sb("rpair", [P, B])
        wn = sb("wn", [P, B, TOP])
        wa = sb("wa", [P, B, TOP])
        gate_w = sb("gate_w", [P, B, TOP])

        gp = [ctx.enter_context(nc.psum_tensor(f"gp{i}", [P, T], F32)) for i in range(PAIRS)]
        up = [ctx.enter_context(nc.psum_tensor(f"up{i}", [P, T], F32)) for i in range(PAIRS)]
        acc = [ctx.enter_context(nc.psum_tensor(f"acc{i}", [P, T], F32)) for i in range(B)]
        fold = [gp[1][:, :P], up[1][:, :P]]
        l0out0 = [acc[0][:, :HALF], gp[2][:, :HALF]]
        l0out1 = acc[1][:, :]
        y1 = [acc[1][:, :HALF], up[1][:, :HALF]]
        l3out0 = gp[1][:, :]
        l3out1 = [gp[2][:, :HALF], up[2][:, :HALF]]

        ld_cond, ld_ab, ld_par, ld_w3 = sem("ld_cond"), sem("ld_ab"), sem("ld_par"), sem("ld_w3")
        ld_x = [sem(f"ld_x{b}") for b in range(B)]
        ld_sh = [sem(f"ld_sh{i}") for i in range(L1_BLOCKS)]
        ld_sk = [sem(f"ld_sk{i}") for i in range(B * TOP)]
        ld_l2 = [sem(f"ld_l2{b}") for b in range(B)]
        s_warm = sem("s_warm")
        s_ident = sem("s_ident")
        s_own = sem("s_own")
        s_wcol = sem("s_wcol")
        s_wbi = sem("s_wbi")
        s_top = sem("s_top")
        s_idx = sem("s_idx")
        s_dif = sem("s_dif")
        s_exp = sem("s_exp")
        s_rt = sem("s_rt")
        s_bsw = sem("s_bsw")
        s_fold = sem("s_fold")
        s_w0 = sem("s_w0")
        s_l0 = sem("s_l0")
        s_x1hi = sem("s_x1hi")
        s_x1lo = sem("s_x1lo")
        s_x1 = sem("s_x1")
        s_x2 = sem("s_x2")
        s_x2hi = sem("s_x2hi")
        s_x2lo = sem("s_x2lo")
        s_x3 = sem("s_x3")
        s_whi = sem("s_whi")
        s_wlov = sem("s_wlov")
        s_wlo = sem("s_wlo")
        s_g = sem("s_g")
        s_u = sem("s_u")
        s_d = sem("s_d")
        s_act = sem("s_act")
        s_h = sem("s_h")
        s_hhi = sem("s_hhi")
        s_hlo = sem("s_hlo")
        s_f3 = sem("s_f3")
        s_l3o = sem("s_l3o")
        s_res0 = sem("s_res0")
        s_res1 = [sem(f"s_res1{i}") for i in range(2)]
        s_out = sem("s_out")

        def raw_piece(p):
            if p < L1_BLOCKS:
                return raw_shared[:, p, :]
            q = p - L1_BLOCKS
            if q < B * TOP * L1_BLOCKS:
                i = q % L1_BLOCKS
                return raw_skill[:, q // L1_BLOCKS, i * PIECE:(i + 1) * PIECE]
            q -= B * TOP * L1_BLOCKS
            i = q % L2_BLOCKS
            return raw_l2[:, q // L2_BLOCKS, i * PIECE:(i + 1) * PIECE]

        def wait_piece_loaded(eng, p):
            if p < L1_BLOCKS:
                eng.wait_ge(ld_sh[p], 16)
            elif p < L1_BLOCKS * (1 + B * TOP):
                eng.wait_ge(ld_sk[p // L1_BLOCKS - 1], 16)
            else:
                eng.wait_ge(ld_l2[(p - L1_BLOCKS * (1 + B * TOP)) // L2_BLOCKS], 16)

        block = ctx.enter_context(nc.Block())

        @block.sync
        def _(sp):
            sp.dma_start(condb[:, :, :].rearrange("p b e -> p (b e)"),
                         cond.rearrange("(a b) e -> a (b e)", a=1).to_broadcast([P, B * E])).then_inc(ld_cond, 16)
            sp.dma_start(params[:, :2 * P], l0[:, :2 * P]).then_inc(ld_ab, 16)
            sp.dma_start(params[:, 2 * P:], l0[:, 2 * P:]).then_inc(ld_par, 16)
            sp.dma_start(x0[:, 0, :], x_t[:, 0:T]).then_inc(ld_x[0], 16)
            sp.dma_start(raw_shared[:, 0, :], shared[0]).then_inc(ld_sh[0], 16)
            sp.dma_start(raw_shared[:, 1, :], shared[1]).then_inc(ld_sh[1], 16)
            sp.dma_start(x0[:, 1, :], x_t[:, T:2 * T]).then_inc(ld_x[1], 16)
            for i in range(2, L1_BLOCKS):
                sp.dma_start(raw_shared[:, i, :], shared[i]).then_inc(ld_sh[i], 16)
            sp.wait_ge(s_idx, B)
            for b in range(B):
                for r in range(TOP):
                    e = sp.value_load(idx[0:1, b, r:r + 1], min_val=0, max_val=E - 1)
                    n = b * TOP + r
                    sp.dma_start(raw_skill[:, n, :], skill[bass.ds(e, 1), :, :]).then_inc(ld_sk[n], 16)
                    if n == 0:
                        sp.dma_start(w3in[:, :, :], l3.rearrange("p (g o) -> p g o", o=P)).then_inc(ld_w3, 16)
            for b in range(B):
                e = sp.value_load(idx[0:1, b, 0:1], min_val=0, max_val=E - 1)
                sp.dma_start(raw_l2[:, b, :], l2[bass.ds(e, 1), :, :]).then_inc(ld_l2[b], 16)
            sp.wait_ge(s_res1[1], 1)
            sp.dma_start(out_t[:, T + HALF:], res[:, 1, HALF:]).then_inc(s_out, 16)
            sp.wait_ge(s_out, 16 * 3)

        @block.gpsimd
        def _(pool):
            R = P // E
            pool.memset(own[:, :], 1.0).then_inc(s_own, 1)
            pool.wait_ge(s_own, 1)
            pool.affine_select(out=own[:, :], in_=own[:, :], compare_op=ALU.is_ge, fill=0.0,
                               base=0, pattern=[[-R, E]], channel_multiplier=1).then_inc(s_own, 1)
            pool.wait_ge(s_own, 2)
            pool.affine_select(out=own[:, :], in_=own[:, :], compare_op=ALU.is_ge, fill=0.0,
                               base=R - 1, pattern=[[R, E]], channel_multiplier=-1).then_inc(s_own, 1)
            pool.memset(ident[:, :], 0.0).then_inc(s_ident, 1)
            pool.wait_ge(s_ident, 1)
            pool.affine_select(out=ident[:, :], in_=ident[:, :], compare_op=ALU.not_equal, fill=1.0,
                               base=0, pattern=[[-1, P]], channel_multiplier=1).then_inc(s_ident, 1)
            pool.wait_ge(s_ident, 2)
            pool.wait_ge(ld_par, 16)
            pool.tensor_tensor(w_base_i[:, :], w_base, ident[:, :], ALU.add).then_inc(s_wbi, 1)

            def lo(p):
                pool.wait_ge(s_whi, p + 1)
                pool.tensor_tensor(wlo[:, p, :], raw_piece(p), whi[:, p, :], ALU.subtract).then_inc(s_wlo, 1)

            def layer3_weights():
                G = E // 2
                mask = w3in[:, E:E + 1, :].to_broadcast([P, G, P])
                pool.wait_ge(ld_w3, 16)
                for g in (0, G):
                    yield pool.tensor_tensor(w3in[:, g:g + G, :], w3in[:, g:g + G, :], mask, ALU.mult)
                for b in range(B):
                    for g in (0, G):
                        y = condb[:, b, g:g + G].unsqueeze(2).to_broadcast([P, G, P])
                        yield pool.tensor_tensor(w3sum[:, g:g + G, :], w3in[:, g:g + G, :], y, ALU.mult)
                    n = G
                    while n:
                        yield pool.tensor_tensor(w3sum[:, 0:n, :], w3sum[:, 0:n, :], w3sum[:, n:2 * n, :], ALU.add)
                        n //= 2
                    yield pool.tensor_tensor(w3[:, b, :], w3sum[:, 0, :], ident[:, :], ALU.add)

            def x1_sum(b):
                pool.wait_ge(s_x1lo, 2 + b)
                pool.tensor_tensor(x1[:, b, :], xhi[:, 0, b, :], xlo[:, 0, b, :], ALU.add).then_inc(s_x1, 1)

            for p in range(DVE_LO, L1_BLOCKS):
                lo(p)
            x1_sum(0)
            pool.wait_ge(ld_cond, 16)
            weights = layer3_weights()
            for p in range(L1_BLOCKS, NPIECES):
                lo(p)
                if p == L1_BLOCKS:
                    x1_sum(1)
                step = p - L1_BLOCKS - 1
                if 0 <= step < L3_STEPS:
                    if step:
                        pool.wait_ge(s_f3, step)
                    next(weights).then_inc(s_f3, 1)

        @block.scalar
        def _(sc):
            sc.wait_ge(s_dif, 1)
            sc.activation(ex[:, :, :], dif[:, :, :], ACT.Exp).then_inc(s_exp, 1)
            sc.wait_ge(s_warm, 1)
            sc.activation(tiny[:, 0:1], warm[:, 0:1], ACT.Gelu_apprx_tanh)

            def hi(p):
                wait_piece_loaded(sc, p)
                sc.activation(whi[:, p, :], raw_piece(p), ACT.Copy).then_inc(s_whi, 1)

            hi(0)
            for n in range(2):
                sc.wait_ge(s_l0, n + 1)
                sc.activation(xhi[:, 0, 0, n * HALF:(n + 1) * HALF], l0out0[n], ACT.Identity, bias=bias0)\
                    .then_inc(s_x1hi, 1)
            hi(1)
            hi(2)

            def h_hi(k, t=slice(0, T)):
                sc.wait_ge(s_h, k + 1 + (t.start > 0))
                if k >= HBUFS:
                    sc.wait_ge(s_d, k - HBUFS + 1)
                i = k % HBUFS
                sc.activation(hhi[:, i, t], h[:, i, t], ACT.Copy).then_inc(s_hhi, 1)

            def x2_hi(b):
                sc.wait_ge(s_x2, b + 1)
                sc.activation(xhi[:, 1, b, :], x2[:, b, :], ACT.Copy).then_inc(s_x2hi, 1)

            def wait_act(k):
                sc.wait_ge(s_g, k + 1)
                if k >= 2:
                    sc.wait_ge(s_h, k - 1)

            def gelu(k):
                wait_act(k)
                sc.activation(act[:, k % 2, :], gp[k % PAIRS][:, :], ACT.Gelu_apprx_tanh).then_inc(s_act, 1)

            def silu(k):
                b, j = divmod(k - N1, L2_BLOCKS)
                bias = raw_l2[:, b, L2_BLOCKS * PIECE + j:L2_BLOCKS * PIECE + j + 1]
                wait_act(k)
                sc.activation(act[:, k % 2, :], gp[k % PAIRS][:, :], ACT.Silu, bias=bias).then_inc(s_act, 1)

            for k in range(N1 - 1):
                if k == 2:
                    sc.wait_ge(s_l0, 3)
                    sc.activation(xhi[:, 0, 1, :], l0out1, ACT.Identity, bias=bias0).then_inc(s_x1hi, 1)
                gelu(k)
                if k:
                    h_hi(k - 1)
                if k == 0:
                    hi(3)
                if k + 1 >= L1_BLOCKS:
                    hi(k + 1)
                if k == X2_BLOCK:
                    x2_hi(0)
            h_hi(N1 - 2)
            gelu(N1 - 1)
            sc.activation(tiny[:, 1:2], warm[:, 0:1], ACT.Silu)
            h_hi(N1 - 1)
            silu(N1)
            h_hi(N1)
            silu(N1 + 1)
            x2_hi(1)
            h_hi(N1 + 1)
            silu(N1 + 2)
            h_hi(N1 + 2)
            silu(N1 + 3)
            for i in range(2):
                h_hi(N1 + 3, slice(i * HALF, (i + 1) * HALF))
            sc.wait_ge(s_l3o, 1)
            sc.activation(res[:, 0, :], l3out0, ACT.Identity, bias=bias3).then_inc(s_res0, 1)
            sc.wait_ge(s_res0, 1)
            sc.dma_start(out_t[:, 0:T], res[:, 0, :]).then_inc(s_out, 16)
            sc.wait_ge(s_l3o, 2)
            sc.activation(res[:, 1, :HALF], l3out1[0], ACT.Identity, bias=bias3).then_inc(s_res1[0], 1)
            sc.wait_ge(s_res1[0], 1)
            sc.dma_start(out_t[:, T:T + HALF], res[:, 1, :HALF]).then_inc(s_out, 16)

        @block.tensor
        def _(pe):
            def spin(n):
                for _ in range(n):
                    pe.matmul(up[0][:, 0:P], warm[:, :], warm[:, :], start=True, stop=True)

            pe.wait_ge(s_warm, 1)
            spin(WARM_MATMULS)
            for b in range(B):
                pe.wait_ge(s_bsw, b + 1)
                pe.matmul(fold[b], a_er, bsw[:, b, :], start=True, stop=True).then_inc(s_fold, 1)
            spin(1)
            pe.wait_ge(s_w0, 1)
            pe.wait_ge(ld_x[0], 16)
            for n in range(2):
                pe.matmul(l0out0[n], w0[:, 0, :], x0[:, 0, n * HALF:(n + 1) * HALF],
                          start=True, stop=True).then_inc(s_l0, 1)

            def hi_passes(out, w_hi, w_lo, v_hi, start):
                pe.matmul(out, w_hi, v_hi, start=start, stop=False)
                return pe.matmul(out, w_lo, v_hi, start=False, stop=False)

            def lo_pass(out, w_hi, v_lo, stop):
                return pe.matmul(out, w_hi, v_lo, start=False, stop=stop)

            def gate_up_first():
                x_h, x_l = xhi[:, 0, 0, :], xlo[:, 0, 0, :]
                pe.wait_ge(s_whi, 1)
                pe.wait_ge(s_wlov, 1)
                for n in range(2):
                    if n == 1:
                        pe.wait_ge(s_w0, 2)
                        pe.wait_ge(ld_x[1], 16)
                        pe.matmul(l0out1, w0[:, 1, :], x0[:, 1, :], start=True, stop=True).then_inc(s_l0, 1)
                    t = slice(n * HALF, (n + 1) * HALF)
                    pe.wait_ge(s_x1hi, n + 1)
                    for c, out in ((0, gp[0]), (P, up[0])):
                        pe.matmul(out[:, t], whi[:, 0, c:c + P], x_h[:, t], start=(n == 0), stop=False,
                                  skip_group_check=True)
                        pe.matmul(out[:, t], wlo[:, 0, c:c + P], x_h[:, t], start=False, stop=False,
                                  skip_group_check=True)
                pe.wait_ge(s_x1lo, 2)
                pe.matmul(gp[0][:, :], whi[:, 0, 0:P], x_l, start=False, stop=True, skip_group_check=True)\
                    .then_inc(s_g, 1)
                pe.matmul(up[0][:, :], whi[:, 0, P:2 * P], x_l, start=False, stop=True, skip_group_check=True)\
                    .then_inc(s_u, 1)

            def gate_up(k, fresh_input=False):
                p, b, layer = piece_of(k), BLOCK_BATCH[k], int(k >= N1)
                pe.wait_ge(s_whi, p + 1)
                if p < DVE_LO:
                    pe.wait_ge(s_wlov, p + 1)
                else:
                    pe.wait_ge(s_wlo, p - DVE_LO + 1)
                if layer == 0:
                    pe.wait_ge(s_x1hi, 2 + b)
                else:
                    pe.wait_ge(s_x2hi, b + 1)
                if k >= PAIRS:
                    pe.wait_ge(s_h, k - PAIRS + 1)
                x_h, x_l = xhi[:, layer, b, :], xlo[:, layer, b, :]
                g, u = gp[k % PAIRS][:, :], up[k % PAIRS][:, :]
                w_g, w_u = (whi[:, p, 0:P], wlo[:, p, 0:P]), (whi[:, p, P:2 * P], wlo[:, p, P:2 * P])

                def wait_lo():
                    if layer == 0:
                        pe.wait_ge(s_x1lo, 2 + b)
                    else:
                        pe.wait_ge(s_x2lo, b + 1)

                hi_passes(g, *w_g, x_h, True)
                if fresh_input:
                    hi_passes(u, *w_u, x_h, True)
                    wait_lo()
                    lo_pass(g, w_g[0], x_l, True).then_inc(s_g, 1)
                else:
                    wait_lo()
                    lo_pass(g, w_g[0], x_l, True).then_inc(s_g, 1)
                    hi_passes(u, *w_u, x_h, True)
                lo_pass(u, w_u[0], x_l, True).then_inc(s_u, 1)

            def wait_down(k):
                if k >= N1 and is_first(k):
                    pe.wait_ge(s_x2, BLOCK_BATCH[k] + 1)
                pe.wait_ge(s_hhi, k + 1)

            def down(k):
                p, i, out = piece_of(k), k % HBUFS, acc[BLOCK_BATCH[k]][:, :]
                wait_down(k)
                hi_passes(out, whi[:, p, 2 * P:], wlo[:, p, 2 * P:], hhi[:, i, :], is_first(k))
                pe.wait_ge(s_hlo, k + 1)
                lo_pass(out, whi[:, p, 2 * P:], hlo[:, i, :], is_last(k)).then_inc(s_d, 1)

            def down_by_halves(k):
                p, i = piece_of(k), k % HBUFS
                wait_down(k)
                if is_first(k):
                    pe.wait_ge(s_h, N1 + 2)
                for n in range(2):
                    t = slice(n * HALF, (n + 1) * HALF)
                    if k == N - 1:
                        pe.wait_ge(s_hhi, k + 1 + n)
                    hi_passes(y1[n], whi[:, p, 2 * P:], wlo[:, p, 2 * P:], hhi[:, i, t], is_first(k))
                    pe.wait_ge(s_hlo, k + 1 + (n if k == N - 1 else 0))
                    mm = lo_pass(y1[n], whi[:, p, 2 * P:], hlo[:, i, t], is_last(k))
                    if n or k == N - 1:
                        mm.then_inc(s_d, 1)

            for k in range(N1):
                if k == 0:
                    gate_up_first()
                else:
                    gate_up(k)
                if k >= LAG:
                    down(k - LAG)
            gate_up(N1)
            down(N1 - 2)
            down(N1 - 1)
            gate_up(N1 + 1)
            down(N1)
            gate_up(N1 + 2, fresh_input=True)
            down(N1 + 1)
            gate_up(N1 + 3)
            pe.wait_ge(s_f3, L3_STEPS)
            pe.wait_ge(s_x3, 1)
            pe.matmul(l3out0, w3[:, 0, :], x3[:, 0, :], start=True, stop=True).then_inc(s_l3o, 1)
            down_by_halves(N1 + 2)
            down_by_halves(N1 + 3)
            for n in range(2):
                pe.wait_ge(s_x3, 2 + n)
                pe.matmul(l3out1[n], w3[:, 1, :], x3[:, 1, n * HALF:(n + 1) * HALF],
                          start=True, stop=True).then_inc(s_l3o, 1)

        @block.vector
        def _(ve):
            ve.memset(warm[:, :], 0.0).then_inc(s_warm, 1)
            ve.wait_ge(ld_cond, 16)
            ve.wait_ge(s_own, 3)
            ve.tensor_tensor(picked[:, :, :], condb[:, :, :], own[:, :].unsqueeze(1).to_broadcast([P, B, E]),
                             ALU.mult).then_inc(s_wcol, 1)
            ve.max(top[:, 0, :], condb[:, 0, :]).then_inc(s_top, 1)
            ve.wait_ge(s_wcol, 1)
            ve.tensor_reduce(wcol[:, :], picked[:, :, :], AX.X, ALU.add).then_inc(s_wcol, 1)
            for b in range(1, B):
                ve.max(top[:, b, :], condb[:, b, :]).then_inc(s_top, 1)
            ve.wait_ge(s_top, B)
            ve.tensor_tensor(dif[:, :, :], top[:, :, :], top[:, :, 0:1].to_broadcast([P, B, 8]), ALU.subtract)\
              .then_inc(s_dif, 1)
            for b in range(B):
                ve.max_index(idx[:, b, :], top[:, b, :], condb[:, b, :]).then_inc(s_idx, 1)
            ve.wait_ge(ld_ab, 16)
            for b in range(B):
                ve.wait_ge(s_wcol, 2)
                ve.tensor_scalar(bsw[:, b, :], b_er, wcol[:, b:b + 1], LORA_SCALE, ALU.mult, ALU.mult)\
                  .then_inc(s_bsw, 1)
            for b in range(B):
                ve.wait_ge(s_fold, b + 1)
                ve.wait_ge(s_wbi, 1)
                ve.tensor_tensor(w0[:, b, :], fold[b], w_base_i[:, :], ALU.add).then_inc(s_w0, 1)

            def lo(p):
                ve.wait_ge(s_whi, p + 1)
                ve.tensor_tensor(wlo[:, p, :], raw_piece(p), whi[:, p, :], ALU.subtract).then_inc(s_wlov, 1)

            def x1_lo(n, l0out, out, hi):
                ve.wait_ge(s_x1hi, n)
                ve.scalar_tensor_tensor(out=out, in0=l0out, scalar=bias0, in1=hi, op0=ALU.add, op1=ALU.subtract)\
                  .then_inc(s_x1lo, 1)

            lo(0)
            for n in range(2):
                t = slice(n * HALF, (n + 1) * HALF)
                x1_lo(n + 1, l0out0[n], xlo[:, 0, 0, t], xhi[:, 0, 0, t])
            lo(1)

            def hidden(k, t=slice(0, T)):
                i = k % HBUFS
                ve.wait_ge(s_act, k + 1)
                ve.wait_ge(s_u, k + 1)
                if k >= HBUFS:
                    ve.wait_ge(s_hhi, k - HBUFS + 1)
                    ve.wait_ge(s_hlo, k - HBUFS + 1)
                a, u = act[:, k % 2, t], up[k % PAIRS][:, t]
                if k >= N1:
                    b, j = divmod(k - N1, L2_BLOCKS)
                    c = L2_BLOCKS * PIECE + L2_BLOCKS + j
                    ve.scalar_tensor_tensor(out=h[:, i, t], in0=u, scalar=raw_l2[:, b, c:c + 1], in1=a,
                                            op0=ALU.add, op1=ALU.mult).then_inc(s_h, 1)
                elif expert_of(k) is None:
                    ve.tensor_tensor(h[:, i, t], u, a, ALU.mult).then_inc(s_h, 1)
                else:
                    b, r = expert_of(k)
                    ve.wait_ge(s_rt, ROUTER_STEPS)
                    ve.scalar_tensor_tensor(out=h[:, i, t], in0=u, scalar=gate_w[:, b, r:r + 1], in1=a,
                                            op0=ALU.mult, op1=ALU.mult).then_inc(s_h, 1)

            def h_lo(k, t=slice(0, T)):
                i = k % HBUFS
                ve.wait_ge(s_hhi, k + 1 + (t.start > 0))
                if k >= HBUFS:
                    ve.wait_ge(s_d, k - HBUFS + 1)
                ve.tensor_tensor(hlo[:, i, t], h[:, i, t], hhi[:, i, t], ALU.subtract).then_inc(s_hlo, 1)

            def router_weights():
                ve.wait_ge(s_exp, 1)
                yield ve.tensor_reduce(ssum[:, :], ex[:, :, :], AX.X, ALU.add)
                yield ve.reciprocal(rsum[:, :], ssum[:, :])
                yield ve.tensor_tensor(rw[:, :, :], ex[:, :, 0:TOP],
                                       rsum[:, :].unsqueeze(2).to_broadcast([P, B, TOP]), ALU.mult)
                yield ve.tensor_reduce(pair[:, :], rw[:, :, :], AX.X, ALU.add)
                yield ve.reciprocal(rpair[:, :], pair[:, :])
                yield ve.tensor_tensor(wn[:, :, :], rw[:, :, :],
                                       rpair[:, :].unsqueeze(2).to_broadcast([P, B, TOP]), ALU.mult)
                yield ve.tensor_scalar(wa[:, :, :], wn[:, :, :], W_SCALE, None, ALU.mult)
                yield ve.scalar_tensor_tensor(out=gate_w[:, :, :], in0=wn[:, :, :], scalar=1.0 - W_SCALE,
                                              in1=wa[:, :, :], op0=ALU.mult, op1=ALU.add)

            def x2_sum(b):
                k = N1 - 1 if b else N1 - TOP * L1_BLOCKS - 1
                ve.wait_ge(s_d, k + 1)
                ve.wait_ge(s_x1, b + 1)
                ve.tensor_tensor(x2[:, b, :], acc[b][:, :], x1[:, b, :], ALU.add).then_inc(s_x2, 1)

            def x2_lo(b):
                ve.wait_ge(s_x2hi, b + 1)
                ve.tensor_tensor(xlo[:, 1, b, :], x2[:, b, :], xhi[:, 1, b, :], ALU.subtract).then_inc(s_x2lo, 1)

            def x3_sum(b, y, t):
                c = L2_BLOCKS * PIECE + 2 * L2_BLOCKS
                ve.scalar_tensor_tensor(out=x3[:, b, t], in0=y, scalar=raw_l2[:, b, c:c + 1],
                                        in1=x2[:, b, t], op0=ALU.add, op1=ALU.add).then_inc(s_x3, 1)

            steps = router_weights()
            for k in range(N1):
                if k == 2:
                    x1_lo(3, l0out1, xlo[:, 0, 1, :], xhi[:, 0, 1, :])
                hidden(k)
                if k:
                    h_lo(k - 1)
                if k < ROUTER_STEPS:
                    if k:
                        ve.wait_ge(s_rt, k)
                    next(steps).then_inc(s_rt, 1)
                if k == X2_BLOCK - 1:
                    x2_sum(0)
                if k == X2_BLOCK + 1:
                    x2_lo(0)
            h_lo(N1 - 1)
            hidden(N1)
            x2_sum(1)
            h_lo(N1)
            hidden(N1 + 1)
            x2_lo(1)
            h_lo(N1 + 1)
            hidden(N1 + 2)
            ve.wait_ge(s_d, N1 + 2)
            x3_sum(0, acc[0][:, :], slice(0, T))
            h_lo(N1 + 2)
            halves = [slice(i * HALF, (i + 1) * HALF) for i in range(2)]
            for t in halves:
                hidden(N1 + 3, t)
            for t in halves:
                h_lo(N1 + 3, t)
            for n, t in enumerate(halves):
                ve.wait_ge(s_d, N + n)
                x3_sum(1, y1[n], t)
            ve.wait_ge(s_l3o, 3)
            ve.tensor_scalar(res[:, 1, HALF:], l3out1[1], bias3, None, ALU.add).then_inc(s_res1[1], 1)


def kernel(**inputs):
    import numpy as np
    import concourse.bacc as bacc
    from concourse.bass_utils import run_bass_kernel_spmd

    i = {name: np.asarray(a) for name, a in inputs.items()}

    def gate_up_down(gate, up_, down, blocks):
        lead = gate.shape[:-2]
        g = np.moveaxis(gate.reshape(*lead, P, blocks, P), -2, -3)
        u = np.moveaxis(up_.reshape(*lead, P, blocks, P), -2, -3)
        d = down.reshape(*lead, blocks, P, P)
        return np.concatenate([g, u, d], axis=-1)

    def rows(pieces):
        m = np.moveaxis(pieces, -3, -2)
        return m.reshape(*m.shape[:-2], -1)

    skill = rows(gate_up_down(i["L1_cond_skill_gate"], i["L1_cond_skill_up"], i["L1_cond_skill_down"], L1_BLOCKS))
    shared = gate_up_down(i["L1_cond_shared_gate"], i["L1_cond_shared_up"], i["L1_cond_shared_down"], L1_BLOCKS)
    l2w = rows(gate_up_down(np.swapaxes(i["L2_cond_W_up"], 1, 2), np.swapaxes(i["L2_cond_W_gate"], 1, 2),
                            np.swapaxes(i["L2_cond_W_down"], 1, 2), L2_BLOCKS))
    l2b = [np.swapaxes(i[n].reshape(E, -1, P), 1, 2) for n in ("L2_cond_b_up", "L2_cond_b_gate", "L2_cond_b_down")]
    arrays = {
        "x_t": i["x"].reshape(B * T, P).T,
        "cond": i["cond_8"],
        "l0": np.concatenate([i["L0_cond_As"].reshape(P, P), np.swapaxes(i["L0_cond_Bs"], 1, 2).reshape(P, P),
                              i["L0_cond_W_base"].T, i["L0_cond_b_base"][:, None], i["L3_cond_bias"][:, None]], axis=1),
        "shared": shared,
        "skill": skill,
        "l2": np.concatenate([l2w, *l2b], axis=-1),
        "l3": np.concatenate([np.moveaxis(i["L3_cond_weight"], -1, 0).reshape(P, E * P), i["L3_cond_mask"].T], axis=1),
    }
    arrays = {name: np.ascontiguousarray(a) for name, a in arrays.items()}
    nc = bacc.Bacc("TRN2", target_bir_lowering=False, num_devices=1)
    ins = [nc.dram_tensor(name, a.shape, mybir.dt.from_np(a.dtype), kind="ExternalInput").ap()
           for name, a in arrays.items()]
    out_t = nc.dram_tensor("out_t", (P, B * T), F32, kind="ExternalOutput").ap()
    build(nc, *ins, out_t)
    got = run_bass_kernel_spmd(nc, [arrays], core_ids=[0]).results[0]["out_t"]
    return np.ascontiguousarray(got.T).reshape(B, T, P)
```
